# Optimizing a Trainium2 kernel written in Bass

```python
import numpy as np
import jax
import jax.numpy as jnp

def _softmax(x, axis=-1):
    return jax.nn.softmax(x, axis=axis)

def _gelu(x):
    return jax.nn.gelu(x, approximate=True)

def _silu(x):
    return jax.nn.silu(x)

def _sigmoid(x):
    return jax.nn.sigmoid(x)

def _layernorm(x, axis=-1, eps=1e-05):
    m = jnp.mean(x, axis=axis, keepdims=True)
    v = jnp.var(x, axis=axis, keepdims=True)
    return (x - m) / jnp.sqrt(v + eps)

def _scatter_add(tgt, idx, src, axis=0):
    return tgt.at[idx].add(src)

def _segment_sum(src, seg, n):
    return jax.ops.segment_sum(src, seg, n)
kernel_name = 'mk_flamingo_gated_d1_seqx_r8_60ec2d'

def setup_inputs(seed: int=0):
    np.random.seed(seed)
    _w = jnp.asarray

    def _rec_inputs():
        import jax
        import jax.numpy as jnp
        _rk = jax.random.key(seed)
        x = -0.000125 + 0.9999 * jax.random.normal(jax.random.fold_in(_rk, 1), (32, 56, 256), jnp.float32)
        _lenS = 56 - jax.random.randint(jax.random.fold_in(_rk, 7), (32,), 0, max(1, 56 // 4) + 1, jnp.int32)
        _lenS2 = 1500 - jax.random.randint(jax.random.fold_in(_rk, 8), (32,), 0, max(1, 1500 // 4) + 1, jnp.int32)
        _ctx_2048P = jax.random.normal(jax.random.fold_in(_rk, 11), (32, 16, 256), jnp.float32)
        _ctx_2048c = jax.random.dirichlet(jax.random.fold_in(_rk, 511), 0.3 * jnp.ones((16,), jnp.float32), (32, 1500))
        _ctx_2048t = jnp.einsum('bsk,bkd->bsd', _ctx_2048c, _ctx_2048P)
        _ctx_2048t = _ctx_2048t * jax.lax.rsqrt(jnp.mean(jnp.square(_ctx_2048t)) + 1e-12) * 0.953939
        ctx_2048 = -0.000514642 + 1.00011 * (_ctx_2048t + 0.3 * jax.random.normal(jax.random.fold_in(_rk, 611), (32, 1500, 256), jnp.float32))
        _validS = jnp.arange(56)[None, :] < _lenS[:, None]
        _validS2 = jnp.arange(1500)[None, :] < _lenS2[:, None]
        _causal = jnp.tril(jnp.ones((56, 56), dtype=bool))
        mask_BxS2_bk0 = jnp.logical_not(jnp.broadcast_to(_validS2[:, :], (32, 1500)))
        _g = jax.random.normal(jax.random.fold_in(_rk, 9001), (2, 1), jnp.float32)
        _g = jnp.sign(_g) * jnp.maximum(jnp.abs(_g), 1.0) + (_g == 0) * 1.0
        g_xattn = _g[0]
        g_ffn = _g[1]
        return (x, ctx_2048, mask_BxS2_bk0, g_xattn, g_ffn)
    x, ctx_2048, mask_BxS2_bk0, g_xattn, g_ffn = _rec_inputs()

    def _L0_xattn_setup():
        import jax, jax.numpy as jnp
        import numpy as np
        key = jax.random.key(seed)
        k1, k2, k3 = jax.random.split(key, 3)
        B, S, D, M = (8, 256, 256, 128)
        hidden_states = jax.random.normal(k1, (B, S, D), dtype=jnp.float32)
        memory_tokens = jax.random.normal(k2, (B, M, D), dtype=jnp.float32)
        memory_mask = jax.random.randint(k3, (B, M), 0, 2).astype(jnp.bool_)
        return {'hidden_states': hidden_states, 'memory_tokens': memory_tokens, 'memory_mask': memory_mask}
    _L0_xattn_all = _L0_xattn_setup()
    _L0_xattn_in = {k: v for k, v in _L0_xattn_all.items() if k in ()}
    del _L0_xattn_all

    def _L0_ffn_setup():
        import jax, jax.numpy as jnp
        import numpy as np
        B, S, D, H = (4, 256, 256, 1024)

        def fwht(x):
            orig_shape = x.shape
            n = orig_shape[-1]
            x = x.reshape(-1, n)
            h = 1
            while h < n:
                xb = x.reshape(-1, n // (2 * h), 2, h)
                a = xb[:, :, 0, :]
                b = xb[:, :, 1, :]
                x = jnp.stack([a + b, a - b], axis=2).reshape(-1, n)
                h *= 2
            scale = jnp.asarray(1.0 / np.sqrt(n), dtype=x.dtype)
            return (x * scale).reshape(orig_shape)
        key = jax.random.key(seed)
        kx, k1, k2, k3 = jax.random.split(key, 4)
        x = jax.random.normal(kx, (B, S, D), dtype=jnp.float32)
        W1 = jax.random.normal(k1, (H, D), dtype=jnp.float32) * (1.0 / np.sqrt(D))
        W2 = jax.random.normal(k2, (D, H), dtype=jnp.float32) * (1.0 / np.sqrt(H))
        W3 = jax.random.normal(k3, (H, D), dtype=jnp.float32) * (1.0 / np.sqrt(D))
        return {'x': x, 'W1': W1, 'W2': W2, 'W3': W3}
    _L0_ffn_all = _L0_ffn_setup()
    _L0_ffn_in = {k: v for k, v in _L0_ffn_all.items() if k in ('W1', 'W2', 'W3')}
    del _L0_ffn_all
    return {'x': x, 'ctx_2048': ctx_2048, 'mask_BxS2_bk0': mask_BxS2_bk0, 'g_xattn': g_xattn, 'g_ffn': g_ffn, 'L0_ffn_W1': _L0_ffn_in['W1'], 'L0_ffn_W2': _L0_ffn_in['W2'], 'L0_ffn_W3': _L0_ffn_in['W3']}

def reference(x, ctx_2048, mask_BxS2_bk0, g_xattn, g_ffn, L0_ffn_W1, L0_ffn_W2, L0_ffn_W3):
    import jax
    import jax.numpy as jnp

    def _L0_xattn_ref(hidden_states, memory_tokens, memory_mask):
        import jax, jax.numpy as jnp
        import numpy as np
        B, S, D = hidden_states.shape
        scale = 1.0 / jnp.sqrt(jnp.asarray(D, hidden_states.dtype))
        scores = jnp.einsum('bsd,bmd->bsm', hidden_states, memory_tokens) * scale
        neg_inf = jnp.asarray(-1e+30, scores.dtype)
        scores = jnp.where(memory_mask[:, None, :], scores, neg_inf)
        attn = jax.nn.softmax(scores, axis=-1)
        readout = jnp.einsum('bsm,bmd->bsd', attn, memory_tokens)
        valid_b = jnp.any(memory_mask, axis=-1)
        out = jnp.where(valid_b[:, None, None], readout, jnp.zeros_like(readout))
        return out

    def _L0_ffn_ref(x, W1, W2, W3):
        import jax, jax.numpy as jnp
        import numpy as np
        B, S, D, H = (4, 256, 256, 1024)

        def fwht(x):
            orig_shape = x.shape
            n = orig_shape[-1]
            x = x.reshape(-1, n)
            h = 1
            while h < n:
                xb = x.reshape(-1, n // (2 * h), 2, h)
                a = xb[:, :, 0, :]
                b = xb[:, :, 1, :]
                x = jnp.stack([a + b, a - b], axis=2).reshape(-1, n)
                h *= 2
            scale = jnp.asarray(1.0 / np.sqrt(n), dtype=x.dtype)
            return (x * scale).reshape(orig_shape)
        up_gate = jnp.einsum('bsd,hd->bsh', x, W1)
        up_lin = jnp.einsum('bsd,hd->bsh', x, W3)
        hidden = jax.nn.silu(up_gate) * up_lin
        hidden = fwht(hidden)
        out = jnp.einsum('bsh,dh->bsd', hidden, W2)
        return out
    x = x + jnp.tanh(g_xattn[0]) * _L0_xattn_ref(_layernorm(x, axis=-1), ctx_2048, mask_BxS2_bk0)
    x = x + jnp.tanh(g_ffn[0]) * _L0_ffn_ref(_layernorm(x, axis=-1), L0_ffn_W1, L0_ffn_W2, L0_ffn_W3)
    return x

_drawn_inputs = setup_inputs


def setup_inputs(seed=0):
    import zlib

    import numpy as np

    out = dict(_drawn_inputs(seed))
    spreads = {}
    factors = {}
    for name, (base, spread) in spreads.items():
        noise = np.random.default_rng([zlib.crc32(name.encode()), seed]).standard_normal(out[name].shape)
        drawn = base * np.exp(spread * noise) if base else spread * noise
        out[name] = jnp.asarray(drawn.astype(out[name].dtype))
    for name, factor in factors.items():
        out[name] = (out[name] * factor).astype(out[name].dtype)
    return out
```

```python
from contextlib import ExitStack

import concourse.bass as bass
import concourse.mybir as mybir

ALU = mybir.AluOpType
ACT = mybir.ActivationFunctionType
AX = mybir.AxisListType
F32 = mybir.dt.float32
F32R = mybir.dt.float32r
BF16 = mybir.dt.bfloat16
U8 = mybir.dt.uint8
U32 = mybir.dt.uint32

P = 128
B, S, D = 32, 56, 256
M = 1500
H = 1024
HALF = 64
PAIRS = B // 2
GROUP = 4
GROUPS = PAIRS // GROUP
PT = 2 * S
GT = GROUP * PT
HP = HALF + S
HG = GROUP * HP
KD = D // P
KH = H // P
NCH = 3
CH = M // NCH
MC = -(-M // P)
MFULL = M // P
MTAIL = M - MFULL * P
MPAD = MC * P
ROUND = 4
ROUNDS = MC // ROUND
SCALE = 1.0 / 16.0
NEG = 1e30
EPS = 1e-5
LOWEST = -3.0e38
UP = [[0, 1, 2], [3, 4, 5], [6, 7], []]
DOWN = [[], [], [], [1, 2, 3]]
DOWN_LATE = [[], [], [0], []]


def gated_block(nc, x, mem_rows, mem_tail, mem_t, mask, g_xattn, g_ffn, w13, w2, consts, out):
    ctx = ExitStack()
    with ctx:
        def sb(name, shape, dt):
            return ctx.enter_context(nc.sbuf_tensor(name, shape, dt))

        def bank(name):
            return ctx.enter_context(nc.psum_tensor(name, [P, 512], F32))

        def sem(name):
            return ctx.enter_context(nc.semaphore(name))

        tokens = sb("tokens", [P, PAIRS + 2, D], F32)
        keys_t = sb("keys_t", [P, 4, KD * M], F32)
        rows = sb("rows", [P, 2, MC * D], F32)
        mask_bits = sb("mask_bits", [P, M // 4], U32)
        bias = sb("bias", [P, M], BF16)
        weights = sb("weights", [P, MPAD], F32)
        weights_t = sb("weights_t", [P, MC, P], F32)
        q_t = sb("q_t", [P, KD, P], F32)
        norm1 = sb("norm1", [P, D], F32)
        norm2 = sb("norm2", [P, D], F32)
        ht_hi = sb("ht_hi", [P, 2 * KD * GT], F32R)
        ht_lo = sb("ht_lo", [P, 2 * KD * GT], F32R)
        w13_hi = sb("w13_hi", [P, 2, KD, H], F32R)
        w13_lo = sb("w13_lo", [P, 2, KD, H], F32R)
        w2_hi = sb("w2_hi", [P, KH, D], F32R)
        w2_lo = sb("w2_lo", [P, KH, D], F32R)
        hid_hi = sb("hid_hi", [P, KH * HG + HALF - S], F32R)
        hid_lo = sb("hid_lo", [P, KH * HG + HALF - S], F32R)
        hid = sb("hid", [P, 2, GT], F32)
        gated = sb("gated", [P, GT], F32)
        const_sb = sb("const_sb", [P, 2, P], F32)
        gates = sb("gates", [P, 2], F32)
        gates_tanh = sb("gates_tanh", [P, 2], F32)
        chunk_max = sb("chunk_max", [P, NCH], F32)
        neg_max = sb("neg_max", [P, 1], F32)
        row_sum = sb("row_sum", [P, 1], F32)
        mask_any = sb("mask_any", [P, 1], F32)
        valid = sb("valid", [P, 1], F32)
        inv_sum = sb("inv_sum", [P, 1], F32)
        coef = sb("coef", [P, 1], F32)
        stats = sb("stats", [P, 2, 6], F32)
        mean_var = sb("mean_var", [P, 2, 2], F32)
        var_eps = sb("var_eps", [P, 2], F32)
        minus_half = sb("minus_half", [P, 2], F32)
        rstd = sb("rstd", [P, 2], F32)

        hadamard = const_sb[:, 0, :]
        ident = const_sb[:, 1, :]
        stage = rows[:, :, :].rearrange("p a n -> p (a n)")
        stage13 = stage[:, 0:2 * KD * H]
        stage2 = stage[:, 2 * KD * H:2 * KD * H + KH * D]

        butterfly_out = stage13[:, 0:KH * D].rearrange("p (a d) -> p a d", a=KH)

        score_bank = [bank(f"score_bank{n}") for n in range(NCH)]
        read_bank = bank("read_bank")
        turn_bank = [bank("turn_bank0"), bank("turn_bank1")]
        gate_bank = bank("gate_bank")
        lin_bank = bank("lin_bank")
        down_bank = [gate_bank, lin_bank]

        consts_loaded = sem("consts_loaded")
        gates_loaded = sem("gates_loaded")
        first_x_loaded = sem("first_x_loaded")
        rest_x_loaded = sem("rest_x_loaded")
        w13_loaded = sem("w13_loaded")
        w2_loaded = sem("w2_loaded")
        keys_loaded = [sem(f"keys_loaded{i}") for i in range(4)]
        rows_loaded = [sem(f"rows_loaded{i}") for i in range(2)]
        mask_loaded = sem("mask_loaded")
        pads_zero = sem("pads_zero")
        rest_zero = sem("rest_zero")
        half_set = sem("half_set")
        gates_ready = sem("gates_ready")
        w13_hi_ready = sem("w13_hi_ready")
        w13_lo_ready = sem("w13_lo_ready")
        butterflies = sem("butterflies")
        folded = sem("folded")
        w2_hi_ready = sem("w2_hi_ready")
        w2_lo_ready = sem("w2_lo_ready")
        stats_done = sem("stats_done")
        moments_ready = sem("moments_ready")
        var_eps_ready = sem("var_eps_ready")
        rstd_ready = sem("rstd_ready")
        norm1_ready = sem("norm1_ready")
        norm2_ready = sem("norm2_ready")
        q_turned = sem("q_turned")
        q_ready = sem("q_ready")
        bias_ready = sem("bias_ready")
        scores_ready = sem("scores_ready")
        masked = sem("masked")
        neg_max_ready = sem("neg_max_ready")
        mask_any_ready = sem("mask_any_ready")
        valid_ready = sem("valid_ready")
        inv_sum_ready = sem("inv_sum_ready")
        coef_ready = sem("coef_ready")
        weights_ready = sem("weights_ready")
        weights_turned = sem("weights_turned")
        weights_t_ready = sem("weights_t_ready")
        read_ready = sem("read_ready")
        x2_ready = sem("x2_ready")
        h_turned = sem("h_turned")
        ht_hi_ready = sem("ht_hi_ready")
        ht_lo_ready = sem("ht_lo_ready")
        gate_ready = sem("gate_ready")
        tanh_ready = sem("tanh_ready")
        gated_ready = sem("gated_ready")
        lin_ready = sem("lin_ready")
        hid_ready = sem("hid_ready")
        hid_hi_ready = sem("hid_hi_ready")
        hid_lo_ready = sem("hid_lo_ready")
        down_ready = sem("down_ready")
        out_ready = sem("out_ready")
        stored = sem("stored")

        def turn(j, n):
            return turn_bank[(5 * j + n) % 2]

        def ht_slice(tile, parity, j):
            view = tile[:, bass.ds(parity * (KD * GT), KD * GT)].rearrange("p (k t) -> p k t", k=KD)
            return view[:, :, j * PT:(j + 1) * PT].rearrange("p k (b s) -> p k b s", b=2)

        def tile_columns(tile, i):
            at = tile[:, i * HG:i * HG + 1]
            return bass.AP(at.tensor, at.offset, [at.ap[0], [HP, GROUP], [HALF, 2], [1, S]])

        def columns(run):
            return run.rearrange("p (q b s) -> p q b s", q=GROUP, b=2)

        def turned_h(bank_):
            return bank_[:, 0:KD * P].rearrange("p (k b s) -> p k b s", k=KD, b=2)[:, :, :, 0:S]

        def wait_apart(engine, once, semaphore, value):
            if not isinstance(value, int):
                engine.reg_mov(spare[engine.engine], value)
                value = spare[engine.engine]
            engine.wait_ge(*once)
            engine.wait_ge(semaphore, value)

        spare = {e.engine: e.alloc_register(name="waited_for") for e in (nc.vector, nc.gpsimd)}

        x_pairs = x.rearrange("(p b s) d -> b s p d", b=2, s=S)
        out_pairs = out.rearrange("(p b s) d -> b s p d", b=2, s=S)

        block = ctx.enter_context(nc.Block())

        @block.sync
        def _(sp):
            sp.dma_start(const_sb[:, :, :], consts).then_inc(consts_loaded, 16)
            sp.dma_start(gates[:, 0:1], g_xattn.partition_broadcast(P)).then_inc(gates_loaded, 16)
            sp.dma_start(gates[:, 1:2], g_ffn.partition_broadcast(P)).then_inc(gates_loaded, 16)
            sp.wait_ge(pads_zero, 1)
            for b in range(2):
                sp.dma_start(tokens[HALF * b:HALF * b + S, 0:GROUP, :], x_pairs[b, :, 0:GROUP, :])\
                    .then_inc(first_x_loaded, 16)
            sp.dma_start(stage13, w13).then_inc(w13_loaded, 16)
            sp.dma_start(stage2, w2).then_inc(w2_loaded, 16)

            def load_keys(p, parity):
                for b in range(2):
                    sp.dma_start(keys_t[:, 2 * parity + b, :], mem_t[2 * p + b])\
                        .then_inc(keys_loaded[2 * parity + b], 16)

            def load_rows(p):
                for b in range(2):
                    sp.dma_start(rows[:, b, 0:MFULL * D], mem_rows[2 * p + b])\
                        .then_inc(rows_loaded[b], 16)
                    sp.dma_start(rows[0:MTAIL, b, MFULL * D:MC * D], mem_tail[2 * p + b])\
                        .then_inc(rows_loaded[b], 16)

            def load_mask(p):
                bits = mask[bass.ds(2 * p, 2), :]
                src = bass.AP(bits.tensor, bits.offset, [[M // 4, 2], [0, HALF], [1, M // 4]])
                sp.dma_start(mask_bits[:, :], src).then_inc(mask_loaded, 16)

            load_mask(0)
            load_keys(0, 0)
            load_keys(1, 1)
            sp.wait_ge(rest_zero, 1)
            for b in range(2):
                sp.dma_start(tokens[HALF * b:HALF * b + S, GROUP:PAIRS, :], x_pairs[b, :, GROUP:PAIRS, :])\
                    .then_inc(rest_x_loaded, 16)
            sp.wait_ge(w13_lo_ready, 2)
            sp.wait_ge(folded, KH // 2)
            load_rows(0)

            def after(p, parity):
                sp.wait_ge(bias_ready, p + 1)
                sp.wait_ge(mask_any_ready, p + 1)
                load_mask(p + 1)
                sp.wait_ge(scores_ready, NCH * p + NCH)
                load_keys(p + 2, parity)
                sp.wait_ge(read_ready, p + 1)
                load_rows(p + 1)

            with sp.Fori(0, PAIRS // 2 - 1) as i:
                after(2 * i, 0)
                after(2 * i + 1, 1)
            sp.wait_ge(bias_ready, PAIRS - 1)
            sp.wait_ge(mask_any_ready, PAIRS - 1)
            load_mask(PAIRS - 1)
            sp.wait_ge(read_ready, PAIRS - 1)
            load_rows(PAIRS - 1)

        @block.gpsimd
        def _(pool):
            pool.memset(minus_half[:, :], -0.5).then_inc(half_set, 1)

            def make_bias(p):
                wait_apart(pool, (half_set, 1), mask_loaded, 16 * p + 16)
                pool.tensor_scalar(bias[:, :], mask_bits[:, :].bitcast(U8), -1.0, NEG,
                                   ALU.add, ALU.mult).then_inc(bias_ready, 1)

            def make_rstd(t):
                wait_apart(pool, (half_set, 1), moments_ready, 2 * t + 2)
                pool.tensor_scalar(var_eps[:, :], mean_var[:, :, 1], EPS, None, ALU.add)\
                    .then_inc(var_eps_ready, 1)
                pool.wait_ge(var_eps_ready, t + 1)
                pool.tensor_tensor(rstd[:, :], var_eps[:, :], minus_half[:, :], ALU.pow)\
                    .then_inc(rstd_ready, 1)

            def hid_low(G, i):
                pool.wait_ge(hid_hi_ready, KH * G + i + 1)
                pool.tensor_tensor(tile_columns(hid_lo, i), columns(hid[:, i % 2, :]),
                                   tile_columns(hid_hi, i).bitcast(F32), ALU.subtract)\
                    .then_inc(hid_lo_ready, 1)

            def step(p, j, G, last=False):
                if not last:
                    pool.wait_ge(masked, NCH * p + NCH)
                    make_bias(p + 1)
                if G is not None:
                    for i in UP[j]:
                        hid_low(G, i)
                make_rstd(p + 1)

            make_rstd(0)
            make_bias(0)
            pool.memset(tokens[:, GROUP:PAIRS + 2, :], 0.0).then_inc(rest_zero, 1)
            for t in (hid_hi, hid_lo):
                gaps = t[:, S:KH * HG + HALF - S].bitcast(F32)
                gaps = bass.AP(gaps.tensor, gaps.offset, [gaps.ap[0], [HP, KH * GROUP], [1, HALF - S]])
                pool.memset(gaps, 0.0).then_inc(rest_zero, 1)
                pool.memset(t[:, KH * HG:KH * HG + HALF - S].bitcast(F32), 0.0).then_inc(rest_zero, 1)
            for j in range(GROUP):
                step(j, j, None)
            with pool.Fori(1, GROUPS - 1) as g:
                for j in range(GROUP):
                    step(GROUP * g + j, j, g - 1)
            for j in range(GROUP):
                step(PAIRS - GROUP + j, j, GROUPS - 2, last=j == GROUP - 1)
            for i in range(KH):
                hid_low(GROUPS - 1, i)

        @block.scalar
        def _(act):
            def copy_q(t, bank_):
                act.wait_ge(q_turned, t + 1)
                act.activation(q_t[:, :, :].rearrange("p k t -> p (k t)"), bank_[:, 0:KD * P], ACT.Copy)\
                    .then_inc(q_ready, 1)

            def ht_high(p, j, parity):
                act.wait_ge(h_turned, p + 1)
                act.activation(ht_slice(ht_hi, parity, j), turned_h(turn(j + 1, 0)), ACT.Copy)\
                    .then_inc(ht_hi_ready, 1)

            def tanh(G, i):
                act.wait_ge(gate_ready, KH * G + i + 1)
                act.activation(gated[:, :], gate_bank[:, 0:GT], ACT.Tanh, scale=0.5).then_inc(tanh_ready, 1)

            def hid_high(G, i):
                act.wait_ge(hid_ready, KH * G + i + 1)
                act.activation(tile_columns(hid_hi, i), columns(hid[:, i % 2, :]), ACT.Copy)\
                    .then_inc(hid_hi_ready, 1)

            def store(G):
                act.wait_ge(out_ready, GROUP * G + GROUP)
                for b in range(2):
                    act.dma_start(out_pairs[b, :, bass.ds(GROUP * G, GROUP), :],
                                  tokens[HALF * b:HALF * b + S, bass.ds(GROUP * G, GROUP), :])\
                        .then_inc(stored, 16)

            def copy_weights(p, j, r):
                act.wait_ge(weights_turned, ROUNDS * p + r + 1)
                act.activation(weights_t[:, ROUND * r:ROUND * r + ROUND, :].rearrange("p c t -> p (c t)"),
                               turn(j, 2 + r)[:, :], ACT.Copy).then_inc(weights_t_ready, 1)

            def fold_high():
                for n in range(KH // 2):
                    act.wait_ge(folded, n + 1)
                    act.activation(w2_hi[:, 2 * n:2 * n + 2, :].rearrange("p a d -> p (a d)"),
                                   down_bank[n % 2][:, :], ACT.Copy, scale=1.0 / 32.0).then_inc(w2_hi_ready, 1)

            def step(p, j, G, parity, before=None):
                if before is not None:
                    ht_high(p - 1, (j - 1) % GROUP, before)
                copy_q(p + 1, turn(j, 1))
                todo = list(UP[j]) if G is not None else []
                if todo:
                    tanh(G, todo[0])
                act.wait_ge(neg_max_ready, p + 1)
                act.activation(weights[:, 0:M], weights[:, 0:M], ACT.Exp, bias=neg_max[:, 0:1], scale=1.0,
                               accum_out=row_sum[:, 0:1]).then_inc(weights_ready, 1)
                if before is None:
                    fold_high()
                for n, i in enumerate(todo):
                    if n:
                        tanh(G, i)
                    if n < len(todo) - 1:
                        hid_high(G, i)
                copy_weights(p, j, 0)
                if todo:
                    hid_high(G, todo[-1])
                copy_weights(p, j, 1)
                copy_weights(p, j, 2)

            act.wait_ge(gates_loaded, 32)
            act.activation(gates_tanh[:, :], gates[:, :], ACT.Tanh).then_inc(gates_ready, 1)
            copy_q(0, turn_bank[0])
            act.wait_ge(w13_loaded, 16)
            for n in range(2):
                act.activation(w13_hi[:, n, :, :].rearrange("p k h -> p (k h)"),
                               stage13[:, n * KD * H:(n + 1) * KD * H], ACT.Copy).then_inc(w13_hi_ready, 1)
            for j in range(GROUP):
                step(j, j, None, 0, before=0 if j else None)
            with act.Fori(1, GROUPS) as g:
                for j in range(GROUP):
                    step(GROUP * g + j, j, g - 1, g % 2, before=g % 2 if j else (g + 1) % 2)
                store(g - 1)
            ht_high(PAIRS - 1, GROUP - 1, (GROUPS - 1) % 2)
            for i in range(KH):
                tanh(GROUPS - 1, i)
                hid_high(GROUPS - 1, i)
            store(GROUPS - 1)
            act.wait_ge(stored, 32 * GROUPS)

        @block.tensor
        def _(pe):
            def turn_q(t, bank_):
                pe.wait_ge(norm1_ready, t + 1)
                for k in range(KD):
                    mm = pe.transpose(bank_[:, k * P:(k + 1) * P], norm1[:, k * P:(k + 1) * P], ident)
                mm.then_inc(q_turned, 1)

            def turn_h(p, bank_):
                pe.wait_ge(norm2_ready, p + 1)
                for k in range(KD):
                    mm = pe.transpose(bank_[:, k * P:(k + 1) * P], norm2[:, k * P:(k + 1) * P], ident)
                mm.then_inc(h_turned, 1)

            def scores(p, j, first=False):
                pe.wait_ge(q_ready, p + 1)
                for b in range(2):
                    pe.wait_ge(keys_loaded[2 * (j % 2) + b], 8 * p + 16 - 8 * (j % 2))
                for n in range(NCH):
                    if not first:
                        pe.wait_ge(masked, NCH * p - NCH + n + 1)
                    for k in range(KD):
                        for b in range(2):
                            keys = keys_t[:, 2 * (j % 2) + b, k * M + n * CH:k * M + (n + 1) * CH]
                            mm = pe.matmul(score_bank[n][HALF * b:HALF * b + HALF, 0:CH],
                                           q_t[:, k, HALF * b:HALF * b + HALF], keys,
                                           start=k == 0, stop=k == KD - 1)
                    mm.then_inc(scores_ready, 1)

            def turn_weights(p, j, before):
                pe.wait_ge(weights_ready, p + 1)
                for r in range(ROUNDS):
                    if r == 0 and before:
                        pe.wait_ge(ht_lo_ready, p)
                    if r == 1:
                        pe.wait_ge(q_ready, p + 2)
                    if r == 2:
                        pe.wait_ge(weights_t_ready, ROUNDS * p + 1)
                    for c in range(ROUND):
                        at = (ROUND * r + c) * P
                        mm = pe.transpose(turn(j, 2 + r)[:, c * P:(c + 1) * P], weights[:, at:at + P], ident)
                    mm.then_inc(weights_turned, 1)

            def readout(p, first=False):
                if not first:
                    pe.wait_ge(x2_ready, p)
                for b in range(2):
                    pe.wait_ge(rows_loaded[b], 32 * p + 32)
                for c in range(MC):
                    if c % ROUND == 0:
                        pe.wait_ge(weights_t_ready, ROUNDS * p + c // ROUND + 1)
                    n = P if c < MFULL else MTAIL
                    for b in range(2):
                        mm = pe.matmul(read_bank[HALF * b:HALF * b + HALF, 0:D],
                                       weights_t[0:n, c, HALF * b:HALF * b + HALF],
                                       rows[0:n, b, c * D:(c + 1) * D], start=c == 0, stop=c == MC - 1)
                mm.then_inc(read_ready, 1)

            def up(G, i, parity, first=False):
                if i == 0:
                    pe.wait_ge(ht_lo_ready, GROUP * G + GROUP)
                    pe.wait_ge(w13_lo_ready, 2)
                for m, bank_ in enumerate((gate_bank, lin_bank)):
                    if i == 0 and first:
                        pe.wait_ge(w2_lo_ready, KH // 2)
                    elif i == 0:
                        pe.wait_ge(out_ready, GROUP * G - 1 + m)
                    elif m == 0:
                        pe.wait_ge(gated_ready, KH * G + i)
                    else:
                        pe.wait_ge(hid_ready, KH * G + i)
                    n = 0
                    for k in range(KD):
                        for w, h in ((w13_hi, ht_hi), (w13_hi, ht_lo), (w13_lo, ht_hi)):
                            rhs = h[:, bass.ds(parity * (KD * GT) + k * GT, GT)]
                            mm = pe.matmul(bank_[:, 0:GT], w[:, m, k, i * P:(i + 1) * P], rhs,
                                           start=n == 0, stop=n == 3 * KD - 1)
                            n += 1
                    mm.then_inc((gate_ready, lin_ready)[m], 1)

            def down(G, q):
                if q == 0:
                    pe.wait_ge(rest_zero, 5)
                if q < 2:
                    pe.wait_ge(hid_lo_ready, KH * G + KH)
                else:
                    pe.wait_ge(out_ready, GROUP * G + q - 1)
                n = 0
                for i in range(KH):
                    for h, w in ((hid_hi, w2_hi), (hid_hi, w2_lo), (hid_lo, w2_hi)):
                        at = i * HG + q * HP
                        mm = pe.matmul(down_bank[q % 2][:, 0:D], h[:, at:at + P], w[:, i, :], start=n == 0,
                                       stop=n == 3 * KH - 1)
                        n += 1
                mm.then_inc(down_ready, 1)

            def step(p, j, G, parity, before=True, first_ffn=False):
                scores(p, j, first=not before)
                if before:
                    turn_h(p - 1, turn(j, 0))
                turn_q(p + 1, turn(j, 1))
                if not before:
                    pe.wait_ge(butterflies, 6)
                    for n in range(KH // 2):
                        if n >= 2:
                            pe.wait_ge(w2_lo_ready, n - 1)
                        pe.matmul(down_bank[n % 2][:, :], hadamard, butterfly_out[:, 2 * n:2 * n + 2, :]
                                  .rearrange("p a d -> p (a d)"), start=True, stop=True).then_inc(folded, 1)
                if G is not None:
                    for i in UP[j]:
                        up(G, i, parity, first_ffn)
                    for q in DOWN[j]:
                        down(G, q)
                turn_weights(p, j, before)
                if G is not None:
                    for q in DOWN_LATE[j]:
                        down(G, q)
                readout(p, first=not before)

            pe.wait_ge(consts_loaded, 16)
            turn_q(0, turn_bank[0])
            for j in range(GROUP):
                step(j, j, None, None, before=j > 0)
            for j in range(GROUP):
                step(GROUP + j, j, 0, 0, first_ffn=True)
            with pe.Fori(2, GROUPS) as g:
                for j in range(GROUP):
                    step(GROUP * g + j, j, g - 1, (g + 1) % 2)
            turn_h(PAIRS - 1, turn(GROUP, 0))
            for i in range(KH):
                up(GROUPS - 1, i, (GROUPS - 1) % 2)
            for q in range(GROUP):
                down(GROUPS - 1, q)

        @block.vector
        def _(dve):
            def moments(tile, which, t):
                dve.bn_stats(stats[:, which, :], tile).then_inc(stats_done, 1)
                wait_apart(dve, (pads_zero, 2), stats_done, 2 * t + which + 1)
                dve.bn_aggr(mean_var[:, which, :], stats[:, which, :]).then_inc(moments_ready, 1)

            def normalize(dst, tile, which, done):
                dve.tensor_scalar(dst[:, :], tile, mean_var[:, which, 0:1], rstd[:, which:which + 1],
                                  ALU.subtract, ALU.mult).then_inc(done, 1)

            def tile_of(p):
                return tokens[:, bass.ds(p, 1), :].rearrange("p a d -> p (a d)")

            def mask_and_max(p):
                for n in range(NCH):
                    if n == 0:
                        dve.wait_ge(bias_ready, p + 1)
                    wait_apart(dve, (pads_zero, 2), scores_ready, NCH * p + n + 1)
                    at = slice(n * CH, (n + 1) * CH)
                    dve.tensor_tensor_reduce(weights[:, at], score_bank[n][:, 0:CH], bias[:, at], SCALE, LOWEST,
                                             ALU.add, ALU.max, chunk_max[:, n:n + 1]).then_inc(masked, 1)
                dve.wait_ge(masked, NCH * p + NCH)
                dve.tensor_reduce(neg_max[:, :], chunk_max[:, :], AX.X, ALU.max, negate=True)\
                    .then_inc(neg_max_ready, 1)

            def any_key(p):
                dve.wait_ge(mask_loaded, 16 * p + 16)
                dve.tensor_reduce(mask_any[:, :], mask_bits[:, :], AX.X, ALU.max)\
                    .then_inc(mask_any_ready, 1)
                dve.wait_ge(mask_any_ready, p + 1)
                dve.tensor_scalar(valid[:, :], mask_any[:, :], 1.0, None, ALU.min).then_inc(valid_ready, 1)

            def ht_low(p, j, parity):
                dve.wait_ge(ht_hi_ready, p + 1)
                hi = ht_slice(ht_hi, parity, j).bitcast(F32)
                dve.tensor_tensor(ht_slice(ht_lo, parity, j), turned_h(turn(j + 1, 0)), hi, ALU.subtract)\
                    .then_inc(ht_lo_ready, 1)

            def hidden(G, i):
                dve.wait_ge(tanh_ready, KH * G + i + 1)
                dve.scalar_tensor_tensor(gated[:, :], gated[:, :], 1.0, gate_bank[:, 0:GT], ALU.add, ALU.mult)\
                    .then_inc(gated_ready, 1)
                dve.wait_ge(gated_ready, KH * G + i + 1)
                dve.wait_ge(lin_ready, KH * G + i + 1)
                if i >= 2:
                    dve.wait_ge(hid_lo_ready, KH * G + i - 1)
                dve.scalar_tensor_tensor(hid[:, i % 2, :], gated[:, :], 0.5, lin_bank[:, 0:GT],
                                         ALU.mult, ALU.mult).then_inc(hid_ready, 1)

            def finish(G, q):
                dve.wait_ge(down_ready, GROUP * G + q + 1)
                tile = tile_of(GROUP * G + q)
                dve.scalar_tensor_tensor(tile, down_bank[q % 2][:, 0:D], gates_tanh[:, 1:2], tile,
                                         ALU.mult, ALU.add).then_inc(out_ready, 1)

            def fold_low():
                for n in range(KH // 2):
                    dve.wait_ge(w2_hi_ready, n + 1)
                    at = w2_hi[:, 2 * n:2 * n + 2, :].rearrange("p a d -> p (a d)").bitcast(F32)
                    dve.scalar_tensor_tensor(w2_lo[:, 2 * n:2 * n + 2, :].rearrange("p a d -> p (a d)"),
                                             down_bank[n % 2][:, :], 1.0 / 32.0, at, ALU.mult, ALU.subtract)\
                        .then_inc(w2_lo_ready, 1)

            def step(p, j, G, before=None):
                any_key(p)
                mask_and_max(p)
                if before is None:
                    fold_low()
                if before is not None:
                    ht_low(p - 1, (j - 1) % GROUP, before)
                if G is not None:
                    for i in UP[j]:
                        hidden(G, i)
                    for q in DOWN[j]:
                        finish(G, q)
                dve.wait_ge(weights_ready, p + 1)
                dve.reciprocal(inv_sum[:, :], row_sum[:, :]).then_inc(inv_sum_ready, 1)
                dve.wait_ge(inv_sum_ready, p + 1)
                dve.wait_ge(valid_ready, p + 1)
                dve.scalar_tensor_tensor(coef[:, :], inv_sum[:, :], valid[:, 0:1], gates_tanh[:, 0:1],
                                         ALU.mult, ALU.mult).then_inc(coef_ready, 1)
                if G is not None:
                    for q in DOWN_LATE[j]:
                        finish(G, q)
                dve.wait_ge(coef_ready, p + 1)
                dve.wait_ge(read_ready, p + 1)
                dve.scalar_tensor_tensor(tile_of(p), read_bank[:, 0:D], coef[:, 0:1], tile_of(p),
                                         ALU.mult, ALU.add).then_inc(x2_ready, 1)
                wait_apart(dve, (pads_zero, 2), x2_ready, p + 1)
                moments(tile_of(p), 0, p + 1)
                moments(tile_of(p + 2), 1, p + 1)
                dve.wait_ge(rstd_ready, p + 2)
                normalize(norm2, tile_of(p), 0, norm2_ready)
                normalize(norm1, tile_of(p + 2), 1, norm1_ready)

            dve.memset(tokens[:, 0:GROUP, :], 0.0).then_inc(pads_zero, 1)
            dve.memset(weights[:, M:MPAD], 0.0).then_inc(pads_zero, 1)
            dve.wait_ge(first_x_loaded, 32)
            moments(tile_of(0), 0, 0)
            moments(tile_of(1), 1, 0)
            dve.wait_ge(rstd_ready, 1)
            normalize(norm1, tile_of(0), 0, norm1_ready)
            dve.wait_ge(q_turned, 1)
            normalize(norm1, tile_of(1), 1, norm1_ready)
            for n in range(2):
                dve.wait_ge(w13_hi_ready, n + 1)
                dve.tensor_tensor(w13_lo[:, n, :, :].rearrange("p k h -> p (k h)"),
                                  stage13[:, n * KD * H:(n + 1) * KD * H],
                                  w13_hi[:, n, :, :].rearrange("p k h -> p (k h)").bitcast(F32),
                                  ALU.subtract).then_inc(w13_lo_ready, 1)
            dve.wait_ge(w2_loaded, 16)
            dve.wait_ge(w13_lo_ready, 2)
            spaces = [stage2, stage13[:, 0:KH * D], stage13[:, KH * D:2 * KH * D], stage13[:, 0:KH * D]]
            for s in range(3):
                if s:
                    dve.wait_ge(butterflies, 2 * s)
                a, b = (spaces[n].rearrange("p (u two v) -> p u two v", two=2, v=(1 << s) * D)
                        for n in (s, s + 1))
                for o, op in enumerate((ALU.add, ALU.subtract)):
                    dve.tensor_tensor(b[:, :, o, :], a[:, :, 0, :], a[:, :, 1, :], op).then_inc(butterflies, 1)
            dve.wait_ge(gates_ready, 1)

            for j in range(GROUP):
                if j == 2:
                    dve.wait_ge(rest_x_loaded, 32)
                step(j, j, None, before=0 if j else None)
            with dve.Fori(1, GROUPS) as g:
                for j in range(GROUP):
                    step(GROUP * g + j, j, g - 1, before=g % 2 if j else (g + 1) % 2)
            ht_low(PAIRS - 1, GROUP - 1, (GROUPS - 1) % 2)
            for i in range(KH):
                hidden(GROUPS - 1, i)
            for q in range(GROUP):
                finish(GROUPS - 1, q)


def kernel(x, ctx_2048, mask_BxS2_bk0, g_xattn, g_ffn, L0_ffn_W1, L0_ffn_W2, L0_ffn_W3):
    import numpy as np
    import concourse.bacc as bacc
    from concourse.bass_utils import run_bass_kernel_spmd

    mem = np.ascontiguousarray(ctx_2048)
    w1, w3, w2 = (np.ascontiguousarray(w) for w in (L0_ffn_W1, L0_ffn_W3, L0_ffn_W2))

    def by_width(w):
        return w.T.reshape(KD, P, H).transpose(1, 0, 2)

    h = np.array([[1.0]], np.float32)
    while h.shape[0] < P:
        h = np.block([[h, h], [h, -h]])
    arrays = {
        "x": np.ascontiguousarray(x).reshape(B * S, D),
        "mem_rows": np.ascontiguousarray(mem[:, :MFULL * P].reshape(B, MFULL, P, D).transpose(0, 2, 1, 3))
        .reshape(B, P, MFULL * D),
        "mem_tail": np.ascontiguousarray(mem[:, MFULL * P:]),
        "mem_t": np.ascontiguousarray(mem.reshape(B, M, KD, P).transpose(0, 3, 2, 1)).reshape(B, P, KD * M),
        "mask": np.ascontiguousarray(mask_BxS2_bk0).view(np.uint8).view(np.uint32),
        "g_xattn": np.ascontiguousarray(g_xattn),
        "g_ffn": np.ascontiguousarray(g_ffn),
        "w13": np.ascontiguousarray(np.stack([by_width(w1), by_width(w3)], 1)).reshape(P, 2 * KD * H),
        "w2": np.ascontiguousarray(w2.T.reshape(KH, P, D).transpose(1, 0, 2)).reshape(P, KH * D),
        "consts": np.stack([h, np.eye(P, dtype=np.float32)], 1).astype(np.float32),
    }
    nc = bacc.Bacc("TRN2", target_bir_lowering=False, num_devices=1)
    args = [nc.dram_tensor(name, a.shape, mybir.dt.from_np(a.dtype), kind="ExternalInput").ap()
            for name, a in arrays.items()]
    out = nc.dram_tensor("out", (B * S, D), F32, kind="ExternalOutput").ap()
    gated_block(nc, *args, out)
    r = run_bass_kernel_spmd(nc, [arrays], core_ids=[0])
    return r.results[0]["out"].reshape(B, S, D)
```

```python
from contextlib import ExitStack

import concourse.bass as bass
import concourse.mybir as mybir

ALU = mybir.AluOpType
ACT = mybir.ActivationFunctionType
AX = mybir.AxisListType
F32 = mybir.dt.float32
F32R = mybir.dt.float32r
BF16 = mybir.dt.bfloat16
U8 = mybir.dt.uint8
U32 = mybir.dt.uint32

P = 128
B, S, D = 32, 56, 256
M = 1500
H = 1024
HALF = 64
PAIRS = B // 2
GROUP = 2
GROUPS = PAIRS // GROUP
GT = GROUP * P
FIRST = 4
KD = D // P
KH = H // P
NCH = 3
CH = M // NCH
MC = -(-M // P)
MFULL = M // P
MTAIL = M - MFULL * P
MPAD = MC * P
ROUND = 4
ROUNDS = MC // ROUND
SCALE = 1.0 / 16.0
NEG = 1e30
EPS = 1e-5
LOWEST = -3.0e38
UP = [[0, 1, 2], [4, 5, 6, 7]]
UP_LATE = [[3], []]


def gated_block(nc, x, mem_rows, mem_tail, mem_t, mask, g_xattn, g_ffn, w13, w2, consts, out):
    ctx = ExitStack()
    with ctx:
        def sb(name, shape, dt):
            return ctx.enter_context(nc.sbuf_tensor(name, shape, dt))

        def bank(name):
            return ctx.enter_context(nc.psum_tensor(name, [P, 512], F32))

        def sem(name):
            return ctx.enter_context(nc.semaphore(name))

        tokens = sb("tokens", [P, PAIRS, D], F32)
        keys_t = sb("keys_t", [P, 4, KD * M], F32)
        rows = sb("rows", [P, 4, MC * D], F32)
        mask_bits = sb("mask_bits", [P, M // 4], U32)
        bias = sb("bias", [P, M], BF16)
        weights = sb("weights", [P, MPAD], F32)
        weights_t = sb("weights_t", [P, MC, P], F32)
        q_t = sb("q_t", [P, KD, P], F32)
        norm1 = sb("norm1", [P, D], F32)
        norm2 = sb("norm2", [P, D], F32)
        ht_hi = sb("ht_hi", [P, 2 * KD * GT], F32R)
        ht_lo = sb("ht_lo", [P, 2 * KD * GT], F32R)
        w13_hi = sb("w13_hi", [P, 2, KD, H], F32R)
        w13_lo = sb("w13_lo", [P, 2, KD, H], F32R)
        w2_hi = sb("w2_hi", [P, KH, D], F32R)
        w2_lo = sb("w2_lo", [P, KH, D], F32R)
        hid_hi = sb("hid_hi", [P, KH, GT], F32R)
        hid_lo = sb("hid_lo", [P, KH, GT], F32R)
        hid = sb("hid", [P, 2, GT], F32)
        gated = sb("gated", [P, 2, GT], F32)
        const_sb = sb("const_sb", [P, 2, P], F32)
        gates = sb("gates", [P, 2], F32)
        gates_tanh = sb("gates_tanh", [P, 2], F32)
        chunk_max = sb("chunk_max", [P, NCH], F32)
        neg_max = sb("neg_max", [P, 1], F32)
        row_sum = sb("row_sum", [P, 1], F32)
        mask_any = sb("mask_any", [P, 1], F32)
        valid = sb("valid", [P, 1], F32)
        inv_sum = sb("inv_sum", [P, 1], F32)
        coef = sb("coef", [P, 1], F32)
        stats = sb("stats", [P, 2, 6], F32)
        mean_var = sb("mean_var", [P, 2, 2], F32)
        var_eps = sb("var_eps", [P, 2], F32)
        minus_half = sb("minus_half", [P, 2], F32)
        rstd = sb("rstd", [P, 2], F32)

        hadamard = const_sb[:, 0, :]
        ident = const_sb[:, 1, :]
        stage13 = [rows[:, 2 + n, 0:KD * H] for n in range(2)]
        w2_space = [keys_t[:, 2 + n % 2, 0:KH * D] for n in range(4)]
        butterfly_out = w2_space[3].rearrange("p (a d) -> p a d", a=KH)

        score_bank = [bank(f"score_bank{n}") for n in range(NCH)]
        read_bank = bank("read_bank")
        turn_bank = [bank("turn_bank0"), bank("turn_bank1")]
        hidden_bank = bank("hidden_bank")
        down_bank = bank("down_bank")
        fold_bank = [hidden_bank, down_bank]
        up_bank = [(score_bank[0], score_bank[1]), (score_bank[2], hidden_bank)]

        consts_loaded = sem("consts_loaded")
        gates_loaded = sem("gates_loaded")
        first_x_loaded = sem("first_x_loaded")
        rest_x_loaded = sem("rest_x_loaded")
        w13_loaded = sem("w13_loaded")
        w2_loaded = sem("w2_loaded")
        keys_loaded = [sem(f"keys_loaded{i}") for i in range(4)]
        rows_loaded = [sem(f"rows_loaded{i}") for i in range(4)]
        mask_loaded = sem("mask_loaded")
        pads_zero = sem("pads_zero")
        rest_zero = sem("rest_zero")
        half_set = sem("half_set")
        gates_ready = sem("gates_ready")
        w13_hi_ready = sem("w13_hi_ready")
        w13_lo_ready = sem("w13_lo_ready")
        butterflies = sem("butterflies")
        folded = sem("folded")
        w2_hi_ready = sem("w2_hi_ready")
        w2_lo_ready = sem("w2_lo_ready")
        keys_turned = sem("keys_turned")
        keys_copied = [sem("keys_copied_by_act"), sem("keys_copied_by_dve")]
        stats_done = sem("stats_done")
        moments_ready = sem("moments_ready")
        var_eps_ready = sem("var_eps_ready")
        rstd_ready = sem("rstd_ready")
        norm1_ready = sem("norm1_ready")
        norm2_ready = sem("norm2_ready")
        q_turned = sem("q_turned")
        q_ready = sem("q_ready")
        bias_ready = sem("bias_ready")
        scores_ready = sem("scores_ready")
        masked = sem("masked")
        neg_max_ready = sem("neg_max_ready")
        mask_any_ready = sem("mask_any_ready")
        valid_ready = sem("valid_ready")
        inv_sum_ready = sem("inv_sum_ready")
        coef_ready = sem("coef_ready")
        weights_ready = sem("weights_ready")
        weights_turned = sem("weights_turned")
        weights_t_ready = sem("weights_t_ready")
        read_ready = sem("read_ready")
        x2_ready = sem("x2_ready")
        h_turned = sem("h_turned")
        ht_hi_ready = sem("ht_hi_ready")
        ht_lo_ready = sem("ht_lo_ready")
        gate_ready = sem("gate_ready")
        tanh_ready = sem("tanh_ready")
        gated_ready = sem("gated_ready")
        lin_ready = sem("lin_ready")
        hid_ready = sem("hid_ready")
        hid_hi_ready = sem("hid_hi_ready")
        hid_lo_ready = sem("hid_lo_ready")
        down_ready = sem("down_ready")
        out_ready = sem("out_ready")
        stored = sem("stored")

        def turn(j, n):
            return turn_bank[(5 * j + n) % 2]

        def ht_slice(tile, parity, j):
            view = tile[:, bass.ds(parity * (KD * GT), KD * GT)].rearrange("p (k t) -> p k t", k=KD)
            return view[:, :, j * P:(j + 1) * P]

        def turned_h(bank_):
            return bank_[:, 0:KD * P].rearrange("p (k t) -> p k t", k=KD)

        KEY_ROUNDS = [(b, k, r) for b in range(2) for k in range(KD) for r in range(ROUNDS)]
        key_bank = [hidden_bank, down_bank, turn_bank[1], turn_bank[0]]

        def key_round(n):
            b, k, r = KEY_ROUNDS[n]
            width = min(ROUND * P, M - r * ROUND * P)
            at = k * M + r * ROUND * P
            return keys_t[:, b, at:at + width], key_bank[n % 4][:, 0:width]

        def moments_count(t):
            if isinstance(t, int) and t >= PAIRS - 1:
                return PAIRS + t
            return 2 * t + 2

        def wait_apart(engine, once, semaphore, value):
            if not isinstance(value, int):
                engine.reg_mov(spare[engine.engine], value)
                value = spare[engine.engine]
            engine.wait_ge(*once)
            engine.wait_ge(semaphore, value)

        spare = {e.engine: e.alloc_register(name="waited_for") for e in (nc.vector, nc.gpsimd)}

        x_pairs = x.rearrange("(p b s) d -> b s p d", b=2, s=S)
        out_pairs = out.rearrange("(p b s) d -> b s p d", b=2, s=S)

        block = ctx.enter_context(nc.Block())

        @block.sync
        def _(sp):
            sp.dma_start(const_sb[:, :, :], consts).then_inc(consts_loaded, 16)
            sp.dma_start(gates[:, 0:1], g_xattn.partition_broadcast(P)).then_inc(gates_loaded, 16)
            sp.dma_start(gates[:, 1:2], g_ffn.partition_broadcast(P)).then_inc(gates_loaded, 16)
            sp.wait_ge(pads_zero, 1)
            def load_x(first, end, done):
                for b in range(2):
                    sp.dma_start(tokens[HALF * b:HALF * b + S, first:end, :], x_pairs[b, :, first:end, :])\
                        .then_inc(done, 16)

            def load_keys(p, parity):
                for b in range(2):
                    sp.dma_start(keys_t[:, 2 * parity + b, :], mem_t[2 * p + b])\
                        .then_inc(keys_loaded[2 * parity + b], 16)

            def load_rows(p, parity):
                for b in range(2):
                    slot = 2 * parity + b
                    sp.dma_start(rows[:, slot, 0:MFULL * D], mem_rows[2 * p + b])\
                        .then_inc(rows_loaded[slot], 16)
                    sp.dma_start(rows[0:MTAIL, slot, MFULL * D:MC * D], mem_tail[2 * p + b])\
                        .then_inc(rows_loaded[slot], 16)

            def load_mask(p):
                bits = mask[bass.ds(2 * p, 2), :]
                src = bass.AP(bits.tensor, bits.offset, [[M // 4, 2], [0, HALF], [1, M // 4]])
                sp.dma_start(mask_bits[:, :], src).then_inc(mask_loaded, 16)

            def next_mask(p):
                sp.wait_ge(bias_ready, p + 1)
                sp.wait_ge(mask_any_ready, p + 1)
                load_mask(p + 1)

            def next_keys(p, parity):
                sp.wait_ge(scores_ready, NCH * p + NCH)
                load_keys(p + 2, parity)

            def next_rows(p, parity):
                sp.wait_ge(read_ready, p + 1)
                load_rows(p + 2, parity)

            def after(p, parity):
                next_keys(p, parity)
                next_mask(p + 1)
                next_rows(p, parity)

            load_x(0, FIRST, first_x_loaded)
            load_mask(0)
            load_rows(0, 0)
            sp.dma_start(w2_space[0], w2).then_inc(w2_loaded, 16)
            for n in range(2):
                sp.dma_start(stage13[n], w13[:, n, :]).then_inc(w13_loaded, 16)
            next_mask(0)
            sp.wait_ge(folded, KH // 2)
            load_keys(1, 1)
            next_mask(1)
            sp.wait_ge(w13_lo_ready, 2)
            load_rows(1, 1)
            next_keys(0, 0)
            next_rows(0, 0)
            next_keys(1, 1)
            sp.wait_ge(rest_zero, 1)
            load_x(FIRST, PAIRS, rest_x_loaded)
            next_mask(2)
            next_rows(1, 1)
            with sp.Fori(1, PAIRS // 2 - 1) as i:
                after(2 * i, 0)
                after(2 * i + 1, 1)

        @block.gpsimd
        def _(pool):
            pool.memset(minus_half[:, :], -0.5).then_inc(half_set, 1)

            def make_bias(p):
                wait_apart(pool, (half_set, 1), mask_loaded, 16 * p + 16)
                pool.tensor_scalar(bias[:, :], mask_bits[:, :].bitcast(U8), -1.0, NEG,
                                   ALU.add, ALU.mult).then_inc(bias_ready, 1)

            def make_rstd(t):
                wait_apart(pool, (half_set, 1), moments_ready, moments_count(t))
                pool.tensor_scalar(var_eps[:, :], mean_var[:, :, 1], EPS, None, ALU.add)\
                    .then_inc(var_eps_ready, 1)
                pool.wait_ge(var_eps_ready, t + 1)
                pool.tensor_tensor(rstd[:, :], var_eps[:, :], minus_half[:, :], ALU.pow)\
                    .then_inc(rstd_ready, 1)

            def hid_low(G, i):
                pool.wait_ge(hid_hi_ready, KH * G + i + 1)
                pool.tensor_tensor(hid_lo[:, i, :], hid[:, i % 2, :], hid_hi[:, i, :].bitcast(F32),
                                   ALU.subtract).then_inc(hid_lo_ready, 1)

            def step(p, j, G, last=False):
                if G is not None:
                    for i in UP[j]:
                        hid_low(G, i)
                if not last:
                    pool.wait_ge(masked, NCH * p + NCH)
                    make_bias(p + 1)
                if G is not None:
                    for i in UP_LATE[j]:
                        hid_low(G, i)
                make_rstd(p + 1)

            make_rstd(0)
            make_bias(0)
            pool.memset(tokens[:, FIRST:PAIRS, :], 0.0).then_inc(rest_zero, 1)
            for j in range(GROUP):
                step(j, j, None)
            with pool.Fori(1, GROUPS - 1) as g:
                for j in range(GROUP):
                    step(GROUP * g + j, j, g - 1)
            for j in range(GROUP):
                step(PAIRS - GROUP + j, j, GROUPS - 2, last=j == GROUP - 1)
            for i in range(KH):
                hid_low(GROUPS - 1, i)

        @block.scalar
        def _(act):
            def copy_q(t, bank_):
                act.wait_ge(q_turned, t + 1)
                act.activation(q_t[:, :, :].rearrange("p k t -> p (k t)"), bank_[:, 0:KD * P], ACT.Copy)\
                    .then_inc(q_ready, 1)

            def ht_high(p, j, parity):
                act.wait_ge(h_turned, p + 1)
                act.activation(ht_slice(ht_hi, parity, j), turned_h(turn(j + 1, 0)), ACT.Copy)\
                    .then_inc(ht_hi_ready, 1)

            def tanh(G, i):
                act.wait_ge(gate_ready, KH * G + i + 1)
                act.activation(gated[:, i % 2, :], up_bank[i % 2][0][:, 0:GT], ACT.Tanh, scale=0.5)\
                    .then_inc(tanh_ready, 1)

            def hid_high(G, i):
                act.wait_ge(hid_ready, KH * G + i + 1)
                act.activation(hid_hi[:, i, :], hid[:, i % 2, :], ACT.Copy).then_inc(hid_hi_ready, 1)

            def store(G):
                act.wait_ge(out_ready, GROUP * G + GROUP)
                for b in range(2):
                    act.dma_start(out_pairs[b, :, bass.ds(GROUP * G, GROUP), :],
                                  tokens[HALF * b:HALF * b + S, bass.ds(GROUP * G, GROUP), :])\
                        .then_inc(stored, 16)

            def copy_weights(p, j, r):
                act.wait_ge(weights_turned, ROUNDS * p + r + 1)
                act.activation(weights_t[:, ROUND * r:ROUND * r + ROUND, :].rearrange("p c t -> p (c t)"),
                               turn(j, 2 + r)[:, :], ACT.Copy).then_inc(weights_t_ready, 1)

            def fold_high(pieces):
                for n in pieces:
                    act.wait_ge(folded, n + 1)
                    act.activation(w2_hi[:, 2 * n:2 * n + 2, :].rearrange("p a d -> p (a d)"),
                                   fold_bank[n % 2][:, :], ACT.Copy, scale=1.0 / 32.0).then_inc(w2_hi_ready, 1)

            def split_w13():
                for n in range(2):
                    act.wait_ge(w13_loaded, 32)
                    act.activation(w13_hi[:, n, :, :].rearrange("p k h -> p (k h)"), stage13[n], ACT.Copy)\
                        .then_inc(w13_hi_ready, 1)

            def step(p, j, G, before=None, last=False):
                if before is not None:
                    ht_high(p - 1, (j - 1) % GROUP, before)
                if not last:
                    copy_q(p + 1, turn(j, 1))
                if before is None:
                    split_w13()
                    fold_high(range(0, 2))
                todo = list(UP[j]) if G is not None else []
                if j == 1 and todo:
                    tanh(G, todo[0])
                act.wait_ge(neg_max_ready, p + 1)
                act.activation(weights[:, 0:M], weights[:, 0:M], ACT.Exp, bias=neg_max[:, 0:1], scale=1.0,
                               accum_out=row_sum[:, 0:1]).then_inc(weights_ready, 1)
                if before is None:
                    fold_high(range(2, KH // 2))
                for n, i in enumerate(todo):
                    if n or j == 0:
                        tanh(G, i)
                    if n:
                        hid_high(G, i - 1)
                copy_weights(p, j, 0)
                if todo:
                    hid_high(G, todo[-1])
                copy_weights(p, j, 1)
                copy_weights(p, j, 2)
                if G is not None:
                    for i in UP_LATE[j]:
                        tanh(G, i)
                        hid_high(G, i)

            act.wait_ge(gates_loaded, 32)
            act.activation(gates_tanh[:, :], gates[:, :], ACT.Tanh).then_inc(gates_ready, 1)
            copy_q(0, turn_bank[0])
            for n in range(0, len(KEY_ROUNDS), 2):
                dst, src = key_round(n)
                act.wait_ge(keys_turned, n + 1)
                act.activation(dst, src, ACT.Copy).then_inc(keys_copied[0], 1)
            for j in range(GROUP):
                step(j, j, None, before=0 if j else None)
            step(GROUP, 0, 0, before=0)
            step(GROUP + 1, 1, 0, before=1)
            with act.Fori(2, GROUPS - 1) as g:
                step(GROUP * g, 0, g - 1, before=(g + 1) % 2)
                store(g - 2)
                step(GROUP * g + 1, 1, g - 1, before=g % 2)
            step(PAIRS - 2, 0, GROUPS - 2, before=GROUPS % 2)
            store(GROUPS - 3)
            step(PAIRS - 1, 1, GROUPS - 2, before=(GROUPS - 1) % 2, last=True)
            ht_high(PAIRS - 1, GROUP - 1, (GROUPS - 1) % 2)
            store(GROUPS - 2)
            tanh(GROUPS - 1, 0)
            for i in range(1, KH):
                tanh(GROUPS - 1, i)
                hid_high(GROUPS - 1, i - 1)
            hid_high(GROUPS - 1, KH - 1)
            store(GROUPS - 1)
            act.wait_ge(stored, 32 * GROUPS)

        @block.tensor
        def _(pe):
            def turn_q(t, bank_):
                pe.wait_ge(norm1_ready, t + 1)
                for k in range(KD):
                    mm = pe.transpose(bank_[:, k * P:(k + 1) * P], norm1[:, k * P:(k + 1) * P], ident)
                mm.then_inc(q_turned, 1)

            def turn_h(p, bank_):
                pe.wait_ge(norm2_ready, p + 1)
                for k in range(KD):
                    mm = pe.transpose(bank_[:, k * P:(k + 1) * P], norm2[:, k * P:(k + 1) * P], ident)
                mm.then_inc(h_turned, 1)

            def scores(p, j, first=False):
                pe.wait_ge(q_ready, p + 1)
                if first:
                    for copied in keys_copied:
                        pe.wait_ge(copied, len(KEY_ROUNDS) // 2)
                else:
                    for b in range(2):
                        pe.wait_ge(keys_loaded[2 * j + b], 8 * p + 8 * j)
                for n in range(NCH):
                    if not first:
                        pe.wait_ge(masked, NCH * p - NCH + n + 1)
                    for k in range(KD):
                        for b in range(2):
                            keys = keys_t[:, 2 * (j % 2) + b, k * M + n * CH:k * M + (n + 1) * CH]
                            mm = pe.matmul(score_bank[n][HALF * b:HALF * b + HALF, 0:CH],
                                           q_t[:, k, HALF * b:HALF * b + HALF], keys,
                                           start=k == 0, stop=k == KD - 1)
                    mm.then_inc(scores_ready, 1)

            def turn_weights(p, j, r):
                for c in range(ROUND):
                    at = (ROUND * r + c) * P
                    mm = pe.transpose(turn(j, 2 + r)[:, c * P:(c + 1) * P], weights[:, at:at + P], ident)
                mm.then_inc(weights_turned, 1)

            def readout(p, j, first=False):
                if not first:
                    pe.wait_ge(x2_ready, p)
                for b in range(2):
                    pe.wait_ge(rows_loaded[2 * (j % 2) + b], 16 * p + 32 - 16 * (j % 2))
                for c in range(MC):
                    if c % ROUND == 0:
                        pe.wait_ge(weights_t_ready, ROUNDS * p + c // ROUND + 1)
                    n = P if c < MFULL else MTAIL
                    for b in range(2):
                        mm = pe.matmul(read_bank[HALF * b:HALF * b + HALF, 0:D],
                                       weights_t[0:n, c, HALF * b:HALF * b + HALF],
                                       rows[0:n, 2 * (j % 2) + b, c * D:(c + 1) * D], start=c == 0, stop=c == MC - 1)
                mm.then_inc(read_ready, 1)

            def up(G, i, parity, p=None):
                if p is not None:
                    pe.wait_ge(masked, NCH * p + 2 + i % 2)
                if i == 0:
                    pe.wait_ge(ht_lo_ready, GROUP * G + GROUP)
                    pe.wait_ge(w13_lo_ready, 2)
                if i >= 2:
                    pe.wait_ge(hid_ready, KH * G + i - 1)
                for m in range(2):
                    n = 0
                    for k in range(KD):
                        for w, h in ((w13_hi, ht_hi), (w13_hi, ht_lo), (w13_lo, ht_hi)):
                            rhs = h[:, bass.ds(parity * (KD * GT) + k * GT, GT)]
                            mm = pe.matmul(up_bank[i % 2][m][:, 0:GT],
                                           w[:, m, k, i * P:(i + 1) * P], rhs,
                                           start=n == 0, stop=n == 3 * KD - 1)
                            n += 1
                    mm.then_inc((gate_ready, lin_ready)[m], 1)

            def down(G, q, first=False, bank_=down_bank):
                if not first and bank_ is down_bank:
                    pe.wait_ge(out_ready, GROUP * G + q)
                n = 0
                for h, done, ws in ((hid_hi, hid_hi_ready, (w2_hi, w2_lo)), (hid_lo, hid_lo_ready, (w2_hi,))):
                    for i in range(KH):
                        if i in (0, KH - 2, KH - 1):
                            pe.wait_ge(done, KH * G + max(i + 1, KH - 2))
                        for w in ws:
                            mm = pe.matmul(bank_[:, 0:D], h[:, i, q * P:(q + 1) * P], w[:, i, :],
                                           start=n == 0, stop=n == 3 * KH - 1)
                            n += 1
                mm.then_inc(down_ready, 1)

            def fold():
                pe.wait_ge(butterflies, 6)
                for n in range(KH // 2):
                    if n >= 2:
                        pe.wait_ge(w2_lo_ready, n - 1)
                    pe.matmul(fold_bank[n % 2][:, :], hadamard, butterfly_out[:, 2 * n:2 * n + 2, :]
                              .rearrange("p a d -> p (a d)"), start=True, stop=True).then_inc(folded, 1)

            def step(p, j, G, parity=None, before=True, first_ffn=False, last=False):
                if G is not None and (j or not first_ffn):
                    pe.wait_ge(hid_ready, KH * G + KH // 2 * j)
                scores(p, j, first=not before)
                if before:
                    turn_h(p - 1, turn(j, 0))
                if not last:
                    turn_q(p + 1, turn(j, 1))
                if G is not None:
                    if j == 0 and not first_ffn:
                        down(G - 1, 1)
                    if first_ffn:
                        pe.wait_ge(w2_lo_ready, KH // 2)
                    for n, i in enumerate(UP[j]):
                        up(G, i, parity, p if n < 2 else None)
                if not before:
                    fold()
                pe.wait_ge(weights_ready, p + 1)
                if before:
                    pe.wait_ge(ht_lo_ready, p)
                turn_weights(p, j, 0)
                if not last:
                    pe.wait_ge(q_ready, p + 2)
                turn_weights(p, j, 1)
                if G is not None:
                    for i in UP_LATE[j]:
                        up(G, i, parity)
                    if j == 1:
                        down(G, 0, first_ffn)
                pe.wait_ge(weights_t_ready, ROUNDS * p + 1)
                turn_weights(p, j, 2)
                readout(p, j, first=not before)

            pe.wait_ge(consts_loaded, 16)
            turn_q(0, turn_bank[0])
            for n, (b, k, r) in enumerate(KEY_ROUNDS):
                if k == 0 and r == 0:
                    pe.wait_ge(rows_loaded[b], 32)
                if n == 3:
                    pe.wait_ge(q_ready, 1)
                if n >= 4:
                    pe.wait_ge(keys_copied[n % 2], n // 2 - 1)
                for c in range(ROUND * r, ROUND * r + ROUND):
                    rows_n = P if c < MFULL else MTAIL
                    at = (c % ROUND) * P
                    mm = pe.transpose(key_bank[n % 4][:, at:at + rows_n],
                                      rows[0:rows_n, b, c * D + k * P:c * D + (k + 1) * P],
                                      ident[0:rows_n, 0:rows_n])
                mm.then_inc(keys_turned, 1)
            for j in range(GROUP):
                step(j, j, None, before=j > 0)
            for j in range(GROUP):
                step(GROUP + j, j, 0, 0, first_ffn=True)
            with pe.Fori(2, GROUPS - 1) as g:
                for j in range(GROUP):
                    step(GROUP * g + j, j, g - 1, (g + 1) % 2)
            for j in range(GROUP):
                step(PAIRS - GROUP + j, j, GROUPS - 2, GROUPS % 2, last=j == GROUP - 1)
            down(GROUPS - 2, 1)
            turn_h(PAIRS - 1, turn(GROUP, 0))
            for i in range(KH):
                up(GROUPS - 1, i, (GROUPS - 1) % 2)
            down(GROUPS - 1, 0)
            down(GROUPS - 1, 1, bank_=hidden_bank)

        @block.vector
        def _(dve):
            def moments(tile, which, count):
                dve.bn_stats(stats[:, which, :], tile).then_inc(stats_done, 1)
                wait_apart(dve, (pads_zero, 2), stats_done, count)
                dve.bn_aggr(mean_var[:, which, :], stats[:, which, :]).then_inc(moments_ready, 1)

            def normalize(dst, tile, which, done):
                dve.tensor_scalar(dst[:, :], tile, mean_var[:, which, 0:1], rstd[:, which:which + 1],
                                  ALU.subtract, ALU.mult).then_inc(done, 1)

            def tile_of(p):
                return tokens[:, bass.ds(p, 1), :].rearrange("p a d -> p (a d)")

            def mask_chunks(p, chunks):
                for n in chunks:
                    if n == 0:
                        dve.wait_ge(bias_ready, p + 1)
                    wait_apart(dve, (pads_zero, 2), scores_ready, NCH * p + n + 1)
                    at = slice(n * CH, (n + 1) * CH)
                    dve.tensor_tensor_reduce(weights[:, at], score_bank[n][:, 0:CH], bias[:, at], SCALE, LOWEST,
                                             ALU.add, ALU.max, chunk_max[:, n:n + 1]).then_inc(masked, 1)

            def negative_max(p):
                dve.wait_ge(masked, NCH * p + NCH)
                dve.tensor_reduce(neg_max[:, :], chunk_max[:, :], AX.X, ALU.max, negate=True)\
                    .then_inc(neg_max_ready, 1)

            def any_key(p):
                dve.wait_ge(mask_loaded, 16 * p + 16)
                dve.tensor_reduce(mask_any[:, :], mask_bits[:, :], AX.X, ALU.max)\
                    .then_inc(mask_any_ready, 1)
                dve.wait_ge(mask_any_ready, p + 1)
                dve.tensor_scalar(valid[:, :], mask_any[:, :], 1.0, None, ALU.min).then_inc(valid_ready, 1)

            def ht_low(p, j, parity):
                dve.wait_ge(ht_hi_ready, p + 1)
                hi = ht_slice(ht_hi, parity, j).bitcast(F32)
                dve.tensor_tensor(ht_slice(ht_lo, parity, j), turned_h(turn(j + 1, 0)), hi, ALU.subtract)\
                    .then_inc(ht_lo_ready, 1)

            def hidden(G, i):
                dve.wait_ge(tanh_ready, KH * G + i + 1)
                dve.scalar_tensor_tensor(gated[:, i % 2, :], gated[:, i % 2, :], 1.0, up_bank[i % 2][0][:, 0:GT],
                                         ALU.add, ALU.mult).then_inc(gated_ready, 1)
                dve.wait_ge(gated_ready, KH * G + i + 1)
                dve.wait_ge(lin_ready, KH * G + i + 1)
                if i >= 2:
                    dve.wait_ge(hid_lo_ready, KH * G + i - 1)
                dve.scalar_tensor_tensor(hid[:, i % 2, :], gated[:, i % 2, :], 0.5, up_bank[i % 2][1][:, 0:GT],
                                         ALU.mult, ALU.mult).then_inc(hid_ready, 1)

            def finish(G, q, bank_=down_bank):
                dve.wait_ge(down_ready, GROUP * G + q + 1)
                tile = tile_of(GROUP * G + q)
                dve.scalar_tensor_tensor(tile, bank_[:, 0:D], gates_tanh[:, 1:2], tile,
                                         ALU.mult, ALU.add).then_inc(out_ready, 1)

            def butterfly():
                dve.wait_ge(w2_loaded, 16)
                for s in range(3):
                    if s:
                        dve.wait_ge(butterflies, 2 * s)
                    a, b = (w2_space[n].rearrange("p (u two v) -> p u two v", two=2, v=(1 << s) * D)
                            for n in (s, s + 1))
                    for o, op in enumerate((ALU.add, ALU.subtract)):
                        dve.tensor_tensor(b[:, :, o, :], a[:, :, 0, :], a[:, :, 1, :], op).then_inc(butterflies, 1)

            def fold_low():
                for n in range(KH // 2):
                    dve.wait_ge(w2_hi_ready, n + 1)
                    at = w2_hi[:, 2 * n:2 * n + 2, :].rearrange("p a d -> p (a d)").bitcast(F32)
                    dve.scalar_tensor_tensor(w2_lo[:, 2 * n:2 * n + 2, :].rearrange("p a d -> p (a d)"),
                                             fold_bank[n % 2][:, :], 1.0 / 32.0, at, ALU.mult, ALU.subtract)\
                        .then_inc(w2_lo_ready, 1)

            def split_w13():
                for n in range(2):
                    dve.wait_ge(w13_hi_ready, n + 1)
                    dve.tensor_tensor(w13_lo[:, n, :, :].rearrange("p k h -> p (k h)"), stage13[n],
                                      w13_hi[:, n, :, :].rearrange("p k h -> p (k h)").bitcast(F32),
                                      ALU.subtract).then_inc(w13_lo_ready, 1)

            def step(p, j, G, before=None, first_ffn=False, ahead=True, ahead_before=True, last=False):
                if before is None:
                    butterfly()
                mask_chunks(p, range(0, 1))
                if before is not None:
                    dve.wait_ge(rstd_ready, p + 1)
                    normalize(norm2, tile_of(p - 1), 0, norm2_ready)
                    if ahead_before:
                        normalize(norm1, tile_of(p + 1), 1, norm1_ready)
                mask_chunks(p, range(1, NCH))
                negative_max(p)
                if before is None:
                    fold_low()
                    split_w13()
                else:
                    ht_low(p - 1, (j - 1) % GROUP, before)
                if G is not None:
                    if j == 0 and not first_ffn:
                        finish(G - 1, 1)
                    for i in UP[j]:
                        hidden(G, i)
                dve.wait_ge(weights_ready, p + 1)
                dve.reciprocal(inv_sum[:, :], row_sum[:, :]).then_inc(inv_sum_ready, 1)
                dve.wait_ge(inv_sum_ready, p + 1)
                dve.wait_ge(valid_ready, p + 1)
                dve.scalar_tensor_tensor(coef[:, :], inv_sum[:, :], valid[:, 0:1], gates_tanh[:, 0:1],
                                         ALU.mult, ALU.mult).then_inc(coef_ready, 1)
                if not last:
                    dve.wait_ge(coef_ready, p + 1)
                    any_key(p + 1)
                if G is not None:
                    for i in UP_LATE[j]:
                        hidden(G, i)
                    if j == 1:
                        finish(G, 0)
                dve.wait_ge(coef_ready, p + 1)
                dve.wait_ge(read_ready, p + 1)
                dve.scalar_tensor_tensor(tile_of(p), read_bank[:, 0:D], coef[:, 0:1], tile_of(p),
                                         ALU.mult, ALU.add).then_inc(x2_ready, 1)
                wait_apart(dve, (pads_zero, 2), x2_ready, p + 1)
                count = moments_count(p + 1)
                moments(tile_of(p), 0, count - 1 if ahead else count)
                if first_ffn:
                    dve.wait_ge(rest_x_loaded, 32)
                if ahead:
                    moments(tile_of(p + 2), 1, count)

            dve.memset(tokens[:, 0:FIRST, :], 0.0).then_inc(pads_zero, 1)
            dve.memset(weights[:, M:MPAD], 0.0).then_inc(pads_zero, 1)
            dve.wait_ge(first_x_loaded, 32)
            moments(tile_of(0), 0, 1)
            moments(tile_of(1), 1, 2)
            dve.wait_ge(rstd_ready, 1)
            normalize(norm1, tile_of(0), 0, norm1_ready)
            dve.wait_ge(q_turned, 1)
            normalize(norm1, tile_of(1), 1, norm1_ready)
            any_key(0)
            for n in range(1, len(KEY_ROUNDS), 2):
                dst, src = key_round(n)
                dve.wait_ge(keys_turned, n + 1)
                dve.tensor_copy(dst, src).then_inc(keys_copied[1], 1)
            dve.wait_ge(gates_ready, 1)

            for j in range(GROUP):
                step(j, j, None, before=0 if j else None)
            step(GROUP, 0, 0, before=0, first_ffn=True)
            step(GROUP + 1, 1, 0, before=1)
            with dve.Fori(2, GROUPS - 1) as g:
                step(GROUP * g, 0, g - 1, before=(g + 1) % 2)
                step(GROUP * g + 1, 1, g - 1, before=g % 2)
            step(PAIRS - 2, 0, GROUPS - 2, before=GROUPS % 2, ahead=False)
            step(PAIRS - 1, 1, GROUPS - 2, before=(GROUPS - 1) % 2, ahead=False, ahead_before=False,
                 last=True)
            dve.wait_ge(rstd_ready, PAIRS + 1)
            normalize(norm2, tile_of(PAIRS - 1), 0, norm2_ready)
            finish(GROUPS - 2, 1)
            ht_low(PAIRS - 1, GROUP - 1, (GROUPS - 1) % 2)
            for i in range(KH):
                hidden(GROUPS - 1, i)
            finish(GROUPS - 1, 0)
            finish(GROUPS - 1, 1, bank_=hidden_bank)


def kernel(x, ctx_2048, mask_BxS2_bk0, g_xattn, g_ffn, L0_ffn_W1, L0_ffn_W2, L0_ffn_W3):
    import numpy as np
    import concourse.bacc as bacc
    from concourse.bass_utils import run_bass_kernel_spmd

    mem = np.ascontiguousarray(ctx_2048)
    w1, w3, w2 = (np.ascontiguousarray(w) for w in (L0_ffn_W1, L0_ffn_W3, L0_ffn_W2))

    def by_width(w):
        return w.T.reshape(KD, P, H).transpose(1, 0, 2)

    h = np.array([[1.0]], np.float32)
    while h.shape[0] < P:
        h = np.block([[h, h], [h, -h]])
    arrays = {
        "x": np.ascontiguousarray(x).reshape(B * S, D),
        "mem_rows": np.ascontiguousarray(mem[:, :MFULL * P].reshape(B, MFULL, P, D).transpose(0, 2, 1, 3))
        .reshape(B, P, MFULL * D),
        "mem_tail": np.ascontiguousarray(mem[:, MFULL * P:]),
        "mem_t": np.ascontiguousarray(mem.reshape(B, M, KD, P).transpose(0, 3, 2, 1)).reshape(B, P, KD * M),
        "mask": np.ascontiguousarray(mask_BxS2_bk0).view(np.uint8).view(np.uint32),
        "g_xattn": np.ascontiguousarray(g_xattn),
        "g_ffn": np.ascontiguousarray(g_ffn),
        "w13": np.ascontiguousarray(np.stack([by_width(w1), by_width(w3)], 1)).reshape(P, 2, KD * H),
        "w2": np.ascontiguousarray(w2.T.reshape(KH, P, D).transpose(1, 0, 2)).reshape(P, KH * D),
        "consts": np.stack([h, np.eye(P, dtype=np.float32)], 1).astype(np.float32),
    }
    nc = bacc.Bacc("TRN2", target_bir_lowering=False, num_devices=1)
    args = [nc.dram_tensor(name, a.shape, mybir.dt.from_np(a.dtype), kind="ExternalInput").ap()
            for name, a in arrays.items()]
    out = nc.dram_tensor("out", (B * S, D), F32, kind="ExternalOutput").ap()
    gated_block(nc, *args, out)
    r = run_bass_kernel_spmd(nc, [arrays], core_ids=[0])
    return r.results[0]["out"].reshape(B, S, D)
```

```python
from contextlib import ExitStack

import concourse.bass as bass
import concourse.mybir as mybir

ALU = mybir.AluOpType
ACT = mybir.ActivationFunctionType
AX = mybir.AxisListType
F32 = mybir.dt.float32
F32R = mybir.dt.float32r
BF16 = mybir.dt.bfloat16
U8 = mybir.dt.uint8
U32 = mybir.dt.uint32

P = 128
B, S, D = 32, 56, 256
M = 1500
H = 1024
HALF = 64
PAIRS = B // 2
GROUP = 2
GROUPS = PAIRS // GROUP
GT = GROUP * P
FIRST = 6
KD = D // P
KH = H // P
NCH = 3
CH = M // NCH
MC = -(-M // P)
MFULL = M // P
MTAIL = M - MFULL * P
MPAD = MC * P
ROUND = 4
ROUNDS = MC // ROUND
SCALE = 1.0 / 16.0
NEG = 1e30
EPS = 1e-5
LOWEST = -3.0e38
UP = [[0, 1, 2], [4, 5, 6, 7]]
UP_LATE = [[3], []]


def gated_block(nc, x, mem_rows, mem_tail, mem_t, mask, g_xattn, g_ffn, w13, w2, consts, out):
    ctx = ExitStack()
    with ctx:
        def sb(name, shape, dt):
            return ctx.enter_context(nc.sbuf_tensor(name, shape, dt))

        def bank(name):
            return ctx.enter_context(nc.psum_tensor(name, [P, 512], F32))

        def sem(name):
            return ctx.enter_context(nc.semaphore(name))

        tokens = sb("tokens", [P, PAIRS, D], F32)
        keys_t = sb("keys_t", [P, 4, KD * M], F32)
        rows = sb("rows", [P, 4, MC * D], F32)
        mask_bits = sb("mask_bits", [P, M // 4], U32)
        bias = sb("bias", [P, M], BF16)
        weights = sb("weights", [P, MPAD], F32)
        weights_t = sb("weights_t", [P, MC, P], F32)
        q_t = sb("q_t", [P, KD, P], F32)
        norm1 = sb("norm1", [P, D], F32)
        norm2 = sb("norm2", [P, D], F32)
        ht_hi = sb("ht_hi", [P, 2 * KD * GT], F32R)
        ht_lo = sb("ht_lo", [P, 2 * KD * GT], F32R)
        w13_hi = sb("w13_hi", [P, 2, KD, H], F32R)
        w13_lo = sb("w13_lo", [P, 2, KD, H], F32R)
        w2_hi = sb("w2_hi", [P, KH, D], F32R)
        w2_lo = sb("w2_lo", [P, KH, D], F32R)
        hid_hi = sb("hid_hi", [P, KH, GT], F32R)
        hid_lo = sb("hid_lo", [P, KH, GT], F32R)
        hid = sb("hid", [P, 2, GT], F32)
        gated = sb("gated", [P, 2, GT], F32)
        const_sb = sb("const_sb", [P, 2, P], F32)
        gates = sb("gates", [P, 2], F32)
        gates_tanh = sb("gates_tanh", [P, 2], F32)
        chunk_max = sb("chunk_max", [P, NCH], F32)
        neg_max = sb("neg_max", [P, 1], F32)
        row_sum = sb("row_sum", [P, 1], F32)
        mask_any = sb("mask_any", [P, 1], F32)
        valid = sb("valid", [P, 1], F32)
        inv_sum = sb("inv_sum", [P, 1], F32)
        coef = sb("coef", [P, 1], F32)
        stats = sb("stats", [P, 2, 6], F32)
        mean_var = sb("mean_var", [P, 2, 2], F32)
        var_eps = sb("var_eps", [P, 2], F32)
        minus_half = sb("minus_half", [P, 2], F32)
        rstd = sb("rstd", [P, 2], F32)

        hadamard = const_sb[:, 0, :]
        ident = const_sb[:, 1, :]
        stage13 = [rows[:, 2 + n, 0:KD * H] for n in range(2)]
        w2_space = [keys_t[:, 2 + n % 2, 0:KH * D] for n in range(4)]
        butterfly_out = w2_space[3].rearrange("p (a d) -> p a d", a=KH)

        score_bank = [bank(f"score_bank{n}") for n in range(NCH)]
        read_bank = bank("read_bank")
        turn_bank = [bank("turn_bank0"), bank("turn_bank1")]
        hidden_bank = bank("hidden_bank")
        down_bank = bank("down_bank")
        fold_bank = score_bank + [read_bank]
        up_bank = [(score_bank[0], score_bank[1]), (score_bank[2], hidden_bank)]

        consts_loaded = sem("consts_loaded")
        gates_loaded = sem("gates_loaded")
        first_x_loaded = sem("first_x_loaded")
        rest_x_loaded = sem("rest_x_loaded")
        w13_loaded = [sem("w1_loaded"), sem("w3_loaded")]
        w2_loaded = sem("w2_loaded")
        keys_loaded = [sem(f"keys_loaded{i}") for i in range(4)]
        rows_loaded = [sem(f"rows_loaded{i}") for i in range(4)]
        first_rows_loaded = sem("first_rows_loaded")
        mask_loaded = sem("mask_loaded")
        pads_zero = sem("pads_zero")
        rest_zero = sem("rest_zero")
        half_set = sem("half_set")
        gates_ready = sem("gates_ready")
        w13_hi_ready = sem("w13_hi_ready")
        w13_lo_ready = sem("w13_lo_ready")
        butterflies = sem("butterflies")
        folded = sem("folded")
        w2_hi_ready = sem("w2_hi_ready")
        w2_lo_ready = sem("w2_lo_ready")
        keys_turned = sem("keys_turned")
        keys_copied = [sem("keys_copied_by_act"), sem("keys_copied_by_dve")]
        stats_done = sem("stats_done")
        moments_ready = sem("moments_ready")
        var_eps_ready = sem("var_eps_ready")
        rstd_ready = sem("rstd_ready")
        norm1_ready = sem("norm1_ready")
        norm2_ready = sem("norm2_ready")
        q_turned = sem("q_turned")
        q_ready = sem("q_ready")
        bias_ready = sem("bias_ready")
        scores_ready = sem("scores_ready")
        masked = sem("masked")
        neg_max_ready = sem("neg_max_ready")
        mask_any_ready = sem("mask_any_ready")
        valid_ready = sem("valid_ready")
        inv_sum_ready = sem("inv_sum_ready")
        coef_ready = sem("coef_ready")
        weights_ready = sem("weights_ready")
        weights_turned = sem("weights_turned")
        weights_t_ready = sem("weights_t_ready")
        read_ready = sem("read_ready")
        x2_ready = sem("x2_ready")
        h_turned = sem("h_turned")
        ht_hi_ready = sem("ht_hi_ready")
        ht_lo_ready = sem("ht_lo_ready")
        gate_ready = sem("gate_ready")
        tanh_ready = sem("tanh_ready")
        gated_ready = sem("gated_ready")
        lin_ready = sem("lin_ready")
        hid_ready = sem("hid_ready")
        hid_hi_ready = sem("hid_hi_ready")
        hid_lo_ready = sem("hid_lo_ready")
        down_ready = sem("down_ready")
        out_ready = sem("out_ready")
        stored = sem("stored")

        def turn(j, n):
            return turn_bank[(5 * j + n) % 2]

        def ht_slice(tile, parity, j):
            view = tile[:, bass.ds(parity * (KD * GT), KD * GT)].rearrange("p (k t) -> p k t", k=KD)
            return view[:, :, j * P:(j + 1) * P]

        def turned_h(bank_):
            return bank_[:, 0:KD * P].rearrange("p (k t) -> p k t", k=KD)

        KEY_ROUNDS = [(b, k, r) for b in range(2) for r in range(ROUNDS) for k in range(KD)]
        BATCH_ROUNDS = KD * ROUNDS
        COPIER = [b * (n % 2) for n, (b, k, r) in enumerate(KEY_ROUNDS)]
        key_bank = [hidden_bank, down_bank, turn_bank[1], turn_bank[0]]

        def key_round(n):
            b, k, r = KEY_ROUNDS[n]
            width = min(ROUND * P, M - r * ROUND * P)
            at = k * M + r * ROUND * P
            return keys_t[:, b, at:at + width], key_bank[n % 4][:, 0:width]

        def moments_count(t):
            if isinstance(t, int) and t >= PAIRS - 1:
                return PAIRS + t
            return 2 * t + 2

        def wait_apart(engine, once, semaphore, value):
            if not isinstance(value, int):
                engine.reg_mov(spare[engine.engine], value)
                value = spare[engine.engine]
            engine.wait_ge(*once)
            engine.wait_ge(semaphore, value)

        spare = {e.engine: e.alloc_register(name="waited_for") for e in (nc.vector, nc.gpsimd)}

        x_pairs = x.rearrange("(p b s) d -> b s p d", b=2, s=S)
        out_pairs = out.rearrange("(p b s) d -> b s p d", b=2, s=S)

        block = ctx.enter_context(nc.Block())

        @block.sync
        def _(sp):
            def load_x(first, end, done):
                for b in range(2):
                    sp.dma_start(tokens[HALF * b:HALF * b + S, first:end, :], x_pairs[b, :, first:end, :])\
                        .then_inc(done, 16)

            def load_keys(p, parity):
                for b in range(2):
                    sp.dma_start(keys_t[:, 2 * parity + b, :], mem_t[2 * p + b])\
                        .then_inc(keys_loaded[2 * parity + b], 16)

            def load_batch_rows(batch, slot, at=0):
                sp.dma_start(rows[:, slot, at:MFULL * D], mem_rows[batch, :, at:MFULL * D])\
                    .then_inc(rows_loaded[slot], 16)
                sp.dma_start(rows[0:MTAIL, slot, MFULL * D:MC * D], mem_tail[batch])\
                    .then_inc(rows_loaded[slot], 16)

            def load_rows(p, parity):
                for b in range(2):
                    load_batch_rows(2 * p + b, 2 * parity + b)

            def load_mask(p):
                bits = mask[bass.ds(2 * p, 2), :]
                src = bass.AP(bits.tensor, bits.offset, [[M // 4, 2], [0, HALF], [1, M // 4]])
                sp.dma_start(mask_bits[:, :], src).then_inc(mask_loaded, 16)

            def next_mask(p):
                sp.wait_ge(bias_ready, p + 1)
                sp.wait_ge(mask_any_ready, p + 1)
                load_mask(p + 1)

            def next_keys(p, parity):
                sp.wait_ge(scores_ready, NCH * p + NCH)
                load_keys(p + 2, parity)

            def next_rows(p, parity):
                sp.wait_ge(read_ready, p + 1)
                load_rows(p + 2, parity)

            def after(p, parity):
                next_keys(p, parity)
                next_mask(p + 1)
                next_rows(p, parity)

            sp.dma_start(const_sb[:, :, :], consts).then_inc(consts_loaded, 16)
            sp.dma_start(w2_space[0], w2).then_inc(w2_loaded, 16)
            sp.dma_start(rows[:, 0, 0:ROUND * D], mem_rows[0, :, 0:ROUND * D]).then_inc(first_rows_loaded, 16)
            load_batch_rows(0, 0, ROUND * D)
            sp.wait_ge(pads_zero, 1)
            load_x(0, FIRST, first_x_loaded)
            load_mask(0)
            load_batch_rows(1, 1)
            sp.dma_start(gates[:, 0:1], g_xattn.partition_broadcast(P)).then_inc(gates_loaded, 16)
            sp.dma_start(gates[:, 1:2], g_ffn.partition_broadcast(P)).then_inc(gates_loaded, 16)
            for n in range(2):
                sp.dma_start(stage13[n], w13[:, n, :]).then_inc(w13_loaded[n], 16)
            sp.wait_ge(folded, KH // 2)
            load_keys(1, 1)
            next_mask(0)
            sp.wait_ge(w13_lo_ready, 2)
            load_rows(1, 1)
            next_mask(1)
            next_keys(0, 0)
            next_rows(0, 0)
            next_keys(1, 1)
            next_mask(2)
            next_rows(1, 1)
            sp.wait_ge(rest_zero, 1)
            load_x(FIRST, PAIRS, rest_x_loaded)
            with sp.Fori(1, PAIRS // 2 - 1) as i:
                after(2 * i, 0)
                after(2 * i + 1, 1)

        @block.gpsimd
        def _(pool):
            pool.memset(minus_half[:, :], -0.5).then_inc(half_set, 1)

            def make_bias(p):
                wait_apart(pool, (half_set, 1), mask_loaded, 16 * p + 16)
                pool.tensor_scalar(bias[:, :], mask_bits[:, :].bitcast(U8), -1.0, NEG,
                                   ALU.add, ALU.mult).then_inc(bias_ready, 1)

            def make_rstd(t):
                wait_apart(pool, (half_set, 1), moments_ready, moments_count(t))
                pool.tensor_scalar(var_eps[:, :], mean_var[:, :, 1], EPS, None, ALU.add)\
                    .then_inc(var_eps_ready, 1)
                pool.wait_ge(var_eps_ready, t + 1)
                pool.tensor_tensor(rstd[:, :], var_eps[:, :], minus_half[:, :], ALU.pow)\
                    .then_inc(rstd_ready, 1)

            def hid_low(G, i):
                pool.wait_ge(hid_hi_ready, KH * G + i + 1)
                pool.tensor_tensor(hid_lo[:, i, :], hid[:, i % 2, :], hid_hi[:, i, :].bitcast(F32),
                                   ALU.subtract).then_inc(hid_lo_ready, 1)

            def step(p, j, G, last=False):
                if G is not None:
                    for i in UP[j]:
                        hid_low(G, i)
                if not last:
                    pool.wait_ge(masked, NCH * p + NCH)
                    make_bias(p + 1)
                if G is not None:
                    for i in UP_LATE[j]:
                        hid_low(G, i)
                make_rstd(p + 1)

            make_rstd(0)
            make_bias(0)
            pool.memset(tokens[:, FIRST:PAIRS, :], 0.0).then_inc(rest_zero, 1)
            for j in range(GROUP):
                step(j, j, None)
            with pool.Fori(1, GROUPS - 1) as g:
                for j in range(GROUP):
                    step(GROUP * g + j, j, g - 1)
            for j in range(GROUP):
                step(PAIRS - GROUP + j, j, GROUPS - 2, last=j == GROUP - 1)
            for i in range(KH):
                hid_low(GROUPS - 1, i)

        @block.scalar
        def _(act):
            def copy_q(t, bank_):
                act.wait_ge(q_turned, t + 1)
                act.activation(q_t[:, :, :].rearrange("p k t -> p (k t)"), bank_[:, 0:KD * P], ACT.Copy)\
                    .then_inc(q_ready, 1)

            def ht_high(p, j, parity):
                act.wait_ge(h_turned, p + 1)
                act.activation(ht_slice(ht_hi, parity, j), turned_h(turn(j + 1, 0)), ACT.Copy)\
                    .then_inc(ht_hi_ready, 1)

            def tanh(G, i):
                act.wait_ge(gate_ready, KH * G + i + 1)
                act.activation(gated[:, i % 2, :], up_bank[i % 2][0][:, 0:GT], ACT.Tanh, scale=0.5)\
                    .then_inc(tanh_ready, 1)

            def hid_high(G, i):
                act.wait_ge(hid_ready, KH * G + i + 1)
                act.activation(hid_hi[:, i, :], hid[:, i % 2, :], ACT.Copy).then_inc(hid_hi_ready, 1)

            def store(first, pairs):
                act.wait_ge(out_ready, first + pairs)
                for b in range(2):
                    act.dma_start(out_pairs[b, :, bass.ds(first, pairs), :],
                                  tokens[HALF * b:HALF * b + S, bass.ds(first, pairs), :])\
                        .then_inc(stored, 16)

            def copy_weights(p, j, r):
                act.wait_ge(weights_turned, ROUNDS * p + r + 1)
                act.activation(weights_t[:, ROUND * r:ROUND * r + ROUND, :].rearrange("p c t -> p (c t)"),
                               turn(j, 2 + r)[:, :], ACT.Copy).then_inc(weights_t_ready, 1)

            def fold_high():
                for n in range(KH // 2):
                    act.wait_ge(folded, n + 1)
                    act.activation(w2_hi[:, 2 * n:2 * n + 2, :].rearrange("p a d -> p (a d)"),
                                   fold_bank[n][:, :], ACT.Copy, scale=1.0 / 32.0).then_inc(w2_hi_ready, 1)

            def split_w13():
                for n in range(2):
                    act.wait_ge(w13_loaded[n], 16)
                    act.activation(w13_hi[:, n, :, :].rearrange("p k h -> p (k h)"), stage13[n], ACT.Copy)\
                        .then_inc(w13_hi_ready, 1)

            def softmax_weights(p):
                act.wait_ge(neg_max_ready, p + 1)
                act.activation(weights[:, 0:M], weights[:, 0:M], ACT.Exp, bias=neg_max[:, 0:1], scale=1.0,
                               accum_out=row_sum[:, 0:1]).then_inc(weights_ready, 1)

            def step(p, j, G, before, last=False):
                ht_high(p - 1, (j - 1) % GROUP, before)
                if not last:
                    copy_q(p + 1, turn(j, 1))
                if j == 1:
                    tanh(G, UP[j][0])
                softmax_weights(p)
                for n, i in enumerate(UP[j]):
                    if n or j == 0:
                        tanh(G, i)
                    if n:
                        hid_high(G, i - 1)
                copy_weights(p, j, 0)
                hid_high(G, UP[j][-1])
                copy_weights(p, j, 1)
                copy_weights(p, j, 2)
                for i in UP_LATE[j]:
                    tanh(G, i)
                    hid_high(G, i)

            for n in range(len(KEY_ROUNDS)):
                if n == BATCH_ROUNDS:
                    fold_high()
                    copy_q(0, down_bank)
                if COPIER[n] == 0:
                    dst, src = key_round(n)
                    act.wait_ge(keys_turned, n + 1)
                    act.activation(dst, src, ACT.Copy).then_inc(keys_copied[0], 1)
            act.wait_ge(gates_loaded, 32)
            act.activation(gates_tanh[:, :], gates[:, :], ACT.Tanh).then_inc(gates_ready, 1)
            split_w13()
            copy_q(1, turn(0, 1))
            for p in range(GROUP):
                softmax_weights(p)
                for r in range(ROUNDS):
                    copy_weights(p, p, r)
            ht_high(0, 0, 0)
            copy_q(2, turn(1, 1))
            step(GROUP, 0, 0, before=0)
            step(GROUP + 1, 1, 0, before=1)
            with act.Fori(2, GROUPS - 1) as g:
                step(GROUP * g, 0, g - 1, before=(g + 1) % 2)
                store(GROUP * (g - 2), GROUP)
                step(GROUP * g + 1, 1, g - 1, before=g % 2)
            step(PAIRS - 2, 0, GROUPS - 2, before=GROUPS % 2)
            store(PAIRS - 3 * GROUP, GROUP)
            step(PAIRS - 1, 1, GROUPS - 2, before=(GROUPS - 1) % 2, last=True)
            ht_high(PAIRS - 1, GROUP - 1, (GROUPS - 1) % 2)
            store(PAIRS - 2 * GROUP, GROUP)
            tanh(GROUPS - 1, 0)
            for i in range(1, KH):
                tanh(GROUPS - 1, i)
                hid_high(GROUPS - 1, i - 1)
            hid_high(GROUPS - 1, KH - 1)
            store(PAIRS - 2, 1)
            store(PAIRS - 1, 1)
            act.wait_ge(stored, 32 * GROUPS + 32)

        @block.tensor
        def _(pe):
            def turn_q(t, bank_):
                pe.wait_ge(norm1_ready, t + 1)
                for k in range(KD):
                    mm = pe.transpose(bank_[:, k * P:(k + 1) * P], norm1[:, k * P:(k + 1) * P], ident)
                mm.then_inc(q_turned, 1)

            def turn_h(p, bank_):
                pe.wait_ge(norm2_ready, p + 1)
                for k in range(KD):
                    mm = pe.transpose(bank_[:, k * P:(k + 1) * P], norm2[:, k * P:(k + 1) * P], ident)
                mm.then_inc(h_turned, 1)

            def scores(p, j, first=False):
                pe.wait_ge(q_ready, p + 1)
                if first:
                    for engine in range(2):
                        pe.wait_ge(keys_copied[engine], COPIER.count(engine))
                else:
                    for b in range(2):
                        pe.wait_ge(keys_loaded[2 * j + b], 8 * p + 8 * j)
                for n in range(NCH):
                    if first:
                        pe.wait_ge(w2_lo_ready, n + 1)
                    else:
                        pe.wait_ge(masked, NCH * p - NCH + n + 1)
                    for k in range(KD):
                        for b in range(2):
                            keys = keys_t[:, 2 * (j % 2) + b, k * M + n * CH:k * M + (n + 1) * CH]
                            mm = pe.matmul(score_bank[n][HALF * b:HALF * b + HALF, 0:CH],
                                           q_t[:, k, HALF * b:HALF * b + HALF], keys,
                                           start=k == 0, stop=k == KD - 1)
                    mm.then_inc(scores_ready, 1)

            def turn_weights(p, j, r):
                for c in range(ROUND):
                    at = (ROUND * r + c) * P
                    mm = pe.transpose(turn(j, 2 + r)[:, c * P:(c + 1) * P], weights[:, at:at + P], ident)
                mm.then_inc(weights_turned, 1)

            def readout(p, j, first=False):
                if first:
                    pe.wait_ge(w2_lo_ready, KH // 2)
                else:
                    pe.wait_ge(x2_ready, p)
                for b in range(2):
                    pe.wait_ge(rows_loaded[2 * (j % 2) + b], 16 * p + 32 - 16 * (j % 2))
                for c in range(MC):
                    if c % ROUND == 0:
                        pe.wait_ge(weights_t_ready, ROUNDS * p + c // ROUND + 1)
                    n = P if c < MFULL else MTAIL
                    for b in range(2):
                        mm = pe.matmul(read_bank[HALF * b:HALF * b + HALF, 0:D],
                                       weights_t[0:n, c, HALF * b:HALF * b + HALF],
                                       rows[0:n, 2 * (j % 2) + b, c * D:(c + 1) * D], start=c == 0, stop=c == MC - 1)
                mm.then_inc(read_ready, 1)

            def up(G, i, parity, p=None):
                if p is not None:
                    pe.wait_ge(masked, NCH * p + 2 + i % 2)
                if i == 0:
                    pe.wait_ge(ht_lo_ready, GROUP * G + GROUP)
                    pe.wait_ge(w13_lo_ready, 2)
                if i >= 2:
                    pe.wait_ge(hid_ready, KH * G + i - 1)
                for m in range(2):
                    n = 0
                    for k in range(KD):
                        for w, h in ((w13_hi, ht_hi), (w13_hi, ht_lo), (w13_lo, ht_hi)):
                            rhs = h[:, bass.ds(parity * (KD * GT) + k * GT, GT)]
                            mm = pe.matmul(up_bank[i % 2][m][:, 0:GT],
                                           w[:, m, k, i * P:(i + 1) * P], rhs,
                                           start=n == 0, stop=n == 3 * KD - 1)
                            n += 1
                    mm.then_inc((gate_ready, lin_ready)[m], 1)

            def down(G, q, first=False, bank_=down_bank):
                if not first and bank_ is down_bank:
                    pe.wait_ge(out_ready, GROUP * G + q)
                n = 0
                for h, done, ws in ((hid_hi, hid_hi_ready, (w2_hi, w2_lo)), (hid_lo, hid_lo_ready, (w2_hi,))):
                    for i in range(KH):
                        if i in (0, KH - 2, KH - 1):
                            pe.wait_ge(done, KH * G + max(i + 1, KH - 2))
                        for w in ws:
                            mm = pe.matmul(bank_[:, 0:D], h[:, i, q * P:(q + 1) * P], w[:, i, :],
                                           start=n == 0, stop=n == 3 * KH - 1)
                            n += 1
                mm.then_inc(down_ready, 1)

            def fold():
                pe.wait_ge(butterflies, 6)
                for n in range(KH // 2):
                    pe.matmul(fold_bank[n][:, :], hadamard, butterfly_out[:, 2 * n:2 * n + 2, :]
                              .rearrange("p a d -> p (a d)"), start=True, stop=True).then_inc(folded, 1)

            def step(p, j, G, parity, first_ffn=False, last=False):
                if j or not first_ffn:
                    pe.wait_ge(hid_ready, KH * G + KH // 2 * j)
                scores(p, j)
                turn_h(p - 1, turn(j, 0))
                if not last:
                    turn_q(p + 1, turn(j, 1))
                if j == 0 and not first_ffn:
                    down(G - 1, 1)
                for n, i in enumerate(UP[j]):
                    up(G, i, parity, p if n < 2 else None)
                pe.wait_ge(weights_ready, p + 1)
                pe.wait_ge(ht_lo_ready, p)
                turn_weights(p, j, 0)
                if not last:
                    pe.wait_ge(q_ready, p + 2)
                turn_weights(p, j, 1)
                for i in UP_LATE[j]:
                    up(G, i, parity)
                if j == 1:
                    down(G, 0, first_ffn)
                pe.wait_ge(weights_t_ready, ROUNDS * p + 1)
                turn_weights(p, j, 2)
                readout(p, j)

            pe.wait_ge(consts_loaded, 16)
            for n, (b, k, r) in enumerate(KEY_ROUNDS):
                if n == BATCH_ROUNDS:
                    fold()
                    pe.wait_ge(keys_copied[0], BATCH_ROUNDS)
                    turn_q(0, down_bank)
                if n == 0:
                    pe.wait_ge(first_rows_loaded, 16)
                elif n in (KD, BATCH_ROUNDS):
                    pe.wait_ge(rows_loaded[b], 32)
                if n == BATCH_ROUNDS + 3:
                    pe.wait_ge(q_ready, 1)
                if n >= 4:
                    pe.wait_ge(keys_copied[COPIER[n - 4]], COPIER[:n - 3].count(COPIER[n - 4]))
                for c in range(ROUND * r, ROUND * r + ROUND):
                    rows_n = P if c < MFULL else MTAIL
                    at = (c % ROUND) * P
                    mm = pe.transpose(key_bank[n % 4][:, at:at + rows_n],
                                      rows[0:rows_n, b, c * D + k * P:c * D + (k + 1) * P],
                                      ident[0:rows_n, 0:rows_n])
                mm.then_inc(keys_turned, 1)
            scores(0, 0, first=True)
            turn_q(1, turn(0, 1))
            for p in range(GROUP):
                pe.wait_ge(weights_ready, p + 1)
                turn_weights(p, p, 0)
                if p == 0:
                    pe.wait_ge(q_ready, 2)
                turn_weights(p, p, 1)
                pe.wait_ge(weights_t_ready, ROUNDS * p + 1)
                turn_weights(p, p, 2)
                if p == 0:
                    scores(1, 1)
                readout(p, p, first=p == 0)
            turn_h(0, turn(1, 0))
            turn_q(2, turn(1, 1))
            for j in range(GROUP):
                step(GROUP + j, j, 0, 0, first_ffn=True)
            with pe.Fori(2, GROUPS - 1) as g:
                for j in range(GROUP):
                    step(GROUP * g + j, j, g - 1, (g + 1) % 2)
            for j in range(GROUP):
                step(PAIRS - GROUP + j, j, GROUPS - 2, GROUPS % 2, last=j == GROUP - 1)
            down(GROUPS - 2, 1)
            turn_h(PAIRS - 1, turn(GROUP, 0))
            for i in range(KH):
                up(GROUPS - 1, i, (GROUPS - 1) % 2)
            down(GROUPS - 1, 0)
            down(GROUPS - 1, 1, bank_=hidden_bank)

        @block.vector
        def _(dve):
            def moments(tile, which, count):
                dve.bn_stats(stats[:, which, :], tile).then_inc(stats_done, 1)
                wait_apart(dve, (pads_zero, 2), stats_done, count)
                dve.bn_aggr(mean_var[:, which, :], stats[:, which, :]).then_inc(moments_ready, 1)

            def normalize(dst, tile, which, done):
                dve.tensor_scalar(dst[:, :], tile, mean_var[:, which, 0:1], rstd[:, which:which + 1],
                                  ALU.subtract, ALU.mult).then_inc(done, 1)

            def tile_of(p):
                return tokens[:, bass.ds(p, 1), :].rearrange("p a d -> p (a d)")

            def mask_chunks(p, chunks):
                for n in chunks:
                    if n == 0:
                        dve.wait_ge(bias_ready, p + 1)
                    wait_apart(dve, (pads_zero, 2), scores_ready, NCH * p + n + 1)
                    at = slice(n * CH, (n + 1) * CH)
                    dve.tensor_tensor_reduce(weights[:, at], score_bank[n][:, 0:CH], bias[:, at], SCALE, LOWEST,
                                             ALU.add, ALU.max, chunk_max[:, n:n + 1]).then_inc(masked, 1)

            def negative_max(p):
                dve.wait_ge(masked, NCH * p + NCH)
                dve.tensor_reduce(neg_max[:, :], chunk_max[:, :], AX.X, ALU.max, negate=True)\
                    .then_inc(neg_max_ready, 1)

            def any_key(p):
                dve.wait_ge(mask_loaded, 16 * p + 16)
                dve.tensor_reduce(mask_any[:, :], mask_bits[:, :], AX.X, ALU.max)\
                    .then_inc(mask_any_ready, 1)
                dve.wait_ge(mask_any_ready, p + 1)
                dve.tensor_scalar(valid[:, :], mask_any[:, :], 1.0, None, ALU.min).then_inc(valid_ready, 1)

            def ht_low(p, j, parity):
                dve.wait_ge(ht_hi_ready, p + 1)
                hi = ht_slice(ht_hi, parity, j).bitcast(F32)
                dve.tensor_tensor(ht_slice(ht_lo, parity, j), turned_h(turn(j + 1, 0)), hi, ALU.subtract)\
                    .then_inc(ht_lo_ready, 1)

            def hidden(G, i):
                dve.wait_ge(tanh_ready, KH * G + i + 1)
                dve.scalar_tensor_tensor(gated[:, i % 2, :], gated[:, i % 2, :], 1.0, up_bank[i % 2][0][:, 0:GT],
                                         ALU.add, ALU.mult).then_inc(gated_ready, 1)
                dve.wait_ge(gated_ready, KH * G + i + 1)
                dve.wait_ge(lin_ready, KH * G + i + 1)
                if i >= 2:
                    dve.wait_ge(hid_lo_ready, KH * G + i - 1)
                dve.scalar_tensor_tensor(hid[:, i % 2, :], gated[:, i % 2, :], 0.5, up_bank[i % 2][1][:, 0:GT],
                                         ALU.mult, ALU.mult).then_inc(hid_ready, 1)

            def finish(G, q, bank_=down_bank):
                dve.wait_ge(down_ready, GROUP * G + q + 1)
                tile = tile_of(GROUP * G + q)
                dve.scalar_tensor_tensor(tile, bank_[:, 0:D], gates_tanh[:, 1:2], tile,
                                         ALU.mult, ALU.add).then_inc(out_ready, 1)

            def butterfly():
                dve.wait_ge(w2_loaded, 16)
                for s in range(3):
                    if s:
                        dve.wait_ge(butterflies, 2 * s)
                    a, b = (w2_space[n].rearrange("p (u two v) -> p u two v", two=2, v=(1 << s) * D)
                            for n in (s, s + 1))
                    for o, op in enumerate((ALU.add, ALU.subtract)):
                        dve.tensor_tensor(b[:, :, o, :], a[:, :, 0, :], a[:, :, 1, :], op).then_inc(butterflies, 1)

            def fold_low():
                for n in range(KH // 2):
                    dve.wait_ge(w2_hi_ready, n + 1)
                    at = w2_hi[:, 2 * n:2 * n + 2, :].rearrange("p a d -> p (a d)").bitcast(F32)
                    dve.scalar_tensor_tensor(w2_lo[:, 2 * n:2 * n + 2, :].rearrange("p a d -> p (a d)"),
                                             fold_bank[n][:, :], 1.0 / 32.0, at, ALU.mult, ALU.subtract)\
                        .then_inc(w2_lo_ready, 1)

            def split_w13(n):
                dve.wait_ge(w13_hi_ready, n + 1)
                dve.tensor_tensor(w13_lo[:, n, :, :].rearrange("p k h -> p (k h)"), stage13[n],
                                  w13_hi[:, n, :, :].rearrange("p k h -> p (k h)").bitcast(F32),
                                  ALU.subtract).then_inc(w13_lo_ready, 1)

            def attention_scale(p, last=False):
                dve.wait_ge(weights_ready, p + 1)
                dve.reciprocal(inv_sum[:, :], row_sum[:, :]).then_inc(inv_sum_ready, 1)
                dve.wait_ge(inv_sum_ready, p + 1)
                dve.wait_ge(valid_ready, p + 1)
                dve.scalar_tensor_tensor(coef[:, :], inv_sum[:, :], valid[:, 0:1], gates_tanh[:, 0:1],
                                         ALU.mult, ALU.mult).then_inc(coef_ready, 1)
                if not last:
                    dve.wait_ge(coef_ready, p + 1)
                    any_key(p + 1)

            def add_attention(p, ahead=True):
                dve.wait_ge(coef_ready, p + 1)
                dve.wait_ge(read_ready, p + 1)
                dve.scalar_tensor_tensor(tile_of(p), read_bank[:, 0:D], coef[:, 0:1], tile_of(p),
                                         ALU.mult, ALU.add).then_inc(x2_ready, 1)
                wait_apart(dve, (pads_zero, 2), x2_ready, p + 1)
                count = moments_count(p + 1)
                moments(tile_of(p), 0, count - 1 if ahead else count)
                if ahead:
                    moments(tile_of(p + 2), 1, count)

            def norm_turn(t, ahead=True):
                dve.wait_ge(rstd_ready, t + 1)
                normalize(norm2, tile_of(t - 1), 0, norm2_ready)
                if ahead:
                    normalize(norm1, tile_of(t + 1), 1, norm1_ready)

            def step(p, j, G, before, first_ffn=False, ahead=True, ahead_before=True, last=False):
                mask_chunks(p, range(0, 1))
                norm_turn(p, ahead_before)
                mask_chunks(p, range(1, NCH))
                negative_max(p)
                ht_low(p - 1, (j - 1) % GROUP, before)
                if j == 0 and not first_ffn:
                    finish(G - 1, 1)
                for i in UP[j]:
                    hidden(G, i)
                attention_scale(p, last)
                for i in UP_LATE[j]:
                    hidden(G, i)
                if j == 1:
                    finish(G, 0)
                add_attention(p, ahead)

            dve.memset(tokens[:, 0:FIRST, :], 0.0).then_inc(pads_zero, 1)
            dve.memset(weights[:, M:MPAD], 0.0).then_inc(pads_zero, 1)
            butterfly()
            dve.wait_ge(first_x_loaded, 32)
            moments(tile_of(0), 0, 1)
            moments(tile_of(1), 1, 2)
            dve.wait_ge(rstd_ready, 1)
            normalize(norm1, tile_of(0), 0, norm1_ready)
            fold_low()
            dve.wait_ge(q_turned, 1)
            normalize(norm1, tile_of(1), 1, norm1_ready)
            for n in range(len(KEY_ROUNDS)):
                if COPIER[n] == 1:
                    dst, src = key_round(n)
                    dve.wait_ge(keys_turned, n + 1)
                    dve.tensor_copy(dst, src).then_inc(keys_copied[1], 1)
            any_key(0)
            dve.wait_ge(gates_ready, 1)
            split_w13(0)
            for p in range(GROUP):
                if p:
                    dve.wait_ge(weights_turned, ROUNDS * p)
                mask_chunks(p, range(NCH))
                negative_max(p)
                if p == 0:
                    split_w13(1)
                else:
                    add_attention(p - 1)
                    norm_turn(p)
                attention_scale(p)
            add_attention(GROUP - 1)
            ht_low(0, 0, 0)
            step(GROUP, 0, 0, before=0, first_ffn=True)
            step(GROUP + 1, 1, 0, before=1)
            dve.wait_ge(rest_x_loaded, 32)
            with dve.Fori(2, GROUPS - 1) as g:
                step(GROUP * g, 0, g - 1, before=(g + 1) % 2)
                step(GROUP * g + 1, 1, g - 1, before=g % 2)
            step(PAIRS - 2, 0, GROUPS - 2, before=GROUPS % 2, ahead=False)
            step(PAIRS - 1, 1, GROUPS - 2, before=(GROUPS - 1) % 2, ahead=False, ahead_before=False,
                 last=True)
            dve.wait_ge(rstd_ready, PAIRS + 1)
            normalize(norm2, tile_of(PAIRS - 1), 0, norm2_ready)
            finish(GROUPS - 2, 1)
            ht_low(PAIRS - 1, GROUP - 1, (GROUPS - 1) % 2)
            for i in range(KH):
                hidden(GROUPS - 1, i)
            finish(GROUPS - 1, 0)
            finish(GROUPS - 1, 1, bank_=hidden_bank)


def kernel(x, ctx_2048, mask_BxS2_bk0, g_xattn, g_ffn, L0_ffn_W1, L0_ffn_W2, L0_ffn_W3):
    import numpy as np
    import concourse.bacc as bacc
    from concourse.bass_utils import run_bass_kernel_spmd

    mem = np.ascontiguousarray(ctx_2048)
    w1, w3, w2 = (np.ascontiguousarray(w) for w in (L0_ffn_W1, L0_ffn_W3, L0_ffn_W2))

    def by_width(w):
        return w.T.reshape(KD, P, H).transpose(1, 0, 2)

    h = np.array([[1.0]], np.float32)
    while h.shape[0] < P:
        h = np.block([[h, h], [h, -h]])
    arrays = {
        "x": np.ascontiguousarray(x).reshape(B * S, D),
        "mem_rows": np.ascontiguousarray(mem[:, :MFULL * P].reshape(B, MFULL, P, D).transpose(0, 2, 1, 3))
        .reshape(B, P, MFULL * D),
        "mem_tail": np.ascontiguousarray(mem[:, MFULL * P:]),
        "mem_t": np.ascontiguousarray(mem.reshape(B, M, KD, P).transpose(0, 3, 2, 1)).reshape(B, P, KD * M),
        "mask": np.ascontiguousarray(mask_BxS2_bk0).view(np.uint8).view(np.uint32),
        "g_xattn": np.ascontiguousarray(g_xattn),
        "g_ffn": np.ascontiguousarray(g_ffn),
        "w13": np.ascontiguousarray(np.stack([by_width(w1), by_width(w3)], 1)).reshape(P, 2, KD * H),
        "w2": np.ascontiguousarray(w2.T.reshape(KH, P, D).transpose(1, 0, 2)).reshape(P, KH * D),
        "consts": np.stack([h, np.eye(P, dtype=np.float32)], 1).astype(np.float32),
    }
    nc = bacc.Bacc("TRN2", target_bir_lowering=False, num_devices=1)
    args = [nc.dram_tensor(name, a.shape, mybir.dt.from_np(a.dtype), kind="ExternalInput").ap()
            for name, a in arrays.items()]
    out = nc.dram_tensor("out", (B * S, D), F32, kind="ExternalOutput").ap()
    gated_block(nc, *args, out)
    r = run_bass_kernel_spmd(nc, [arrays], core_ids=[0])
    return r.results[0]["out"].reshape(B, S, D)
```
